# Optimizing a Trainium2 kernel written in Bass

```python
import numpy as np
import jax
import jax.numpy as jnp

def _softmax(x, axis=-1):
    return jax.nn.softmax(x, axis=axis)

def _gelu(x):
    return jax.nn.gelu(x, approximate=True)

def _silu(x):
    return jax.nn.silu(x)

def _sigmoid(x):
    return jax.nn.sigmoid(x)

def _layernorm(x, axis=-1, eps=1e-05):
    m = jnp.mean(x, axis=axis, keepdims=True)
    v = jnp.var(x, axis=axis, keepdims=True)
    return (x - m) / jnp.sqrt(v + eps)

def _scatter_add(tgt, idx, src, axis=0):
    return tgt.at[idx].add(src)

def _segment_sum(src, seg, n):
    return jax.ops.segment_sum(src, seg, n)
kernel_name = 'mk_perceiver_d1_seqx_r4_b7184f'

def setup_inputs(seed: int=0):
    np.random.seed(seed)
    _w = jnp.asarray

    def _rec_inputs():
        import jax
        import jax.numpy as jnp
        _rk = jax.random.key(seed)
        x = -0.000125 + 0.9999 * jax.random.normal(jax.random.fold_in(_rk, 1), (1, 256, 256), jnp.float32)
        _lenS = 256 - jax.random.randint(jax.random.fold_in(_rk, 7), (1,), 0, max(1, 256 // 4) + 1, jnp.int32)
        _lenS2 = 4096 - jax.random.randint(jax.random.fold_in(_rk, 8), (1,), 0, max(1, 4096 // 4) + 1, jnp.int32)
        _ctx_768P = jax.random.normal(jax.random.fold_in(_rk, 11), (1, 16, 192), jnp.float32)
        _ctx_768c = jax.random.dirichlet(jax.random.fold_in(_rk, 511), 0.3 * jnp.ones((16,), jnp.float32), (1, 4096))
        _ctx_768t = jnp.einsum('bsk,bkd->bsd', _ctx_768c, _ctx_768P)
        _ctx_768t = _ctx_768t * jax.lax.rsqrt(jnp.mean(jnp.square(_ctx_768t)) + 1e-12) * 0.953939
        ctx_768 = 0.00272024 + 0.999456 * (_ctx_768t + 0.3 * jax.random.normal(jax.random.fold_in(_rk, 611), (1, 4096, 192), jnp.float32))
        return (x, ctx_768)
    x, ctx_768 = _rec_inputs()

    def _L0_xattn_setup():
        import jax, jax.numpy as jnp
        import numpy as np
        B, N, M = (8, 1024, 77)
        Q_DIM, CTX_DIM = (256, 192)
        H, D = (16, 64)
        INNER = H * D
        key = jax.random.key(seed)
        ks = jax.random.split(key, 7)
        x = jax.random.normal(ks[0], (B, N, Q_DIM), dtype=jnp.float32)
        context = jax.random.normal(ks[1], (B, M, CTX_DIM), dtype=jnp.float32)
        Wq = jax.random.normal(ks[2], (Q_DIM, INNER), dtype=jnp.float32) * Q_DIM ** (-0.5)
        Wk = jax.random.normal(ks[3], (CTX_DIM, INNER), dtype=jnp.float32) * CTX_DIM ** (-0.5)
        Wv = jax.random.normal(ks[4], (CTX_DIM, INNER), dtype=jnp.float32) * CTX_DIM ** (-0.5)
        Wo = jax.random.normal(ks[5], (INNER, Q_DIM), dtype=jnp.float32) * INNER ** (-0.5)
        bo = jax.random.normal(ks[6], (Q_DIM,), dtype=jnp.float32) * 0.01
        return {'x': x, 'context': context, 'Wq': Wq, 'Wk': Wk, 'Wv': Wv, 'Wo': Wo, 'bo': bo}
    _L0_xattn_all = _L0_xattn_setup()
    _L0_xattn_in = {k: v for k, v in _L0_xattn_all.items() if k in ('Wq', 'Wk', 'Wv', 'Wo', 'bo')}
    del _L0_xattn_all

    def _L0_attn_setup():
        import jax, jax.numpy as jnp
        import numpy as np
        import math
        D = 256
        H = 16
        HEAD_D = D // H
        T = 512
        B = 4
        key = jax.random.key(seed)
        k1, k2, k3 = jax.random.split(key, 3)
        x = jax.random.normal(k1, (B, T, D), dtype=jnp.float32)
        w_attn = jax.random.normal(k2, (D, D + 2 * HEAD_D), dtype=jnp.float32) * (1.0 / math.sqrt(D))
        w_proj = jax.random.normal(k3, (D, D), dtype=jnp.float32) * (1.0 / math.sqrt(D))
        return {'x': x, 'w_attn': w_attn, 'w_proj': w_proj}
    _L0_attn_all = _L0_attn_setup()
    _L0_attn_in = {k: v for k, v in _L0_attn_all.items() if k in ('w_attn', 'w_proj')}
    del _L0_attn_all

    def _L0_ffn_setup():
        import jax, jax.numpy as jnp
        import numpy as np
        BEST_K = 2

        def _expert(xf, w1, w3, w2):
            return jax.nn.silu(xf @ w1) * (xf @ w3) @ w2
        key = jax.random.key(seed)
        ks = jax.random.split(key, 9)
        E, S_sh, D, H = (8, 2, 256, 128)
        B, S = (2, 512)
        w = lambda k, shape: jax.random.normal(k, shape, dtype=jnp.float32) * 0.02
        return {'x': jax.random.normal(ks[0], (B, S, D), dtype=jnp.float32), 'router_w': w(ks[1], (D, E)), 'router_b': jnp.zeros((E,), dtype=jnp.float32), 'routed_w1': w(ks[2], (E, D, H)), 'routed_w3': w(ks[3], (E, D, H)), 'routed_w2': w(ks[4], (E, H, D)), 'shared_w1': w(ks[5], (S_sh, D, H)), 'shared_w3': w(ks[6], (S_sh, D, H)), 'shared_w2': w(ks[7], (S_sh, H, D))}
    _L0_ffn_all = _L0_ffn_setup()
    _L0_ffn_in = {k: v for k, v in _L0_ffn_all.items() if k in ('router_w', 'router_b', 'routed_w1', 'routed_w3', 'routed_w2', 'shared_w1', 'shared_w3', 'shared_w2')}
    del _L0_ffn_all
    return {'x': x, 'ctx_768': ctx_768, 'L0_xattn_Wq': _L0_xattn_in['Wq'], 'L0_xattn_Wk': _L0_xattn_in['Wk'], 'L0_xattn_Wv': _L0_xattn_in['Wv'], 'L0_xattn_Wo': _L0_xattn_in['Wo'], 'L0_xattn_bo': _L0_xattn_in['bo'], 'L0_attn_w_attn': _L0_attn_in['w_attn'], 'L0_attn_w_proj': _L0_attn_in['w_proj'], 'L0_ffn_router_w': _L0_ffn_in['router_w'], 'L0_ffn_router_b': _L0_ffn_in['router_b'], 'L0_ffn_routed_w1': _L0_ffn_in['routed_w1'], 'L0_ffn_routed_w3': _L0_ffn_in['routed_w3'], 'L0_ffn_routed_w2': _L0_ffn_in['routed_w2'], 'L0_ffn_shared_w1': _L0_ffn_in['shared_w1'], 'L0_ffn_shared_w3': _L0_ffn_in['shared_w3'], 'L0_ffn_shared_w2': _L0_ffn_in['shared_w2']}

def reference(x, ctx_768, L0_xattn_Wq, L0_xattn_Wk, L0_xattn_Wv, L0_xattn_Wo, L0_xattn_bo, L0_attn_w_attn, L0_attn_w_proj, L0_ffn_router_w, L0_ffn_router_b, L0_ffn_routed_w1, L0_ffn_routed_w3, L0_ffn_routed_w2, L0_ffn_shared_w1, L0_ffn_shared_w3, L0_ffn_shared_w2):
    import jax
    import jax.numpy as jnp

    def _L0_xattn_ref(x, context, Wq, Wk, Wv, Wo, bo):
        import jax, jax.numpy as jnp
        import numpy as np
        B, N, M = (8, 1024, 77)
        Q_DIM, CTX_DIM = (256, 192)
        H, D = (16, 64)
        INNER = H * D
        scale = D ** (-0.5)

        def heads(t):
            b, s, _ = t.shape
            return t.reshape(b, s, H, D).transpose(0, 2, 1, 3)
        q = heads(x @ Wq)
        k = heads(context @ Wk)
        v = heads(context @ Wv)
        scores = jnp.einsum('bhid,bhjd->bhij', q, k) * scale
        attn = jax.nn.softmax(scores, axis=-1)
        out = jnp.einsum('bhij,bhjd->bhid', attn, v)
        out = out.transpose(0, 2, 1, 3).reshape(x.shape[0], x.shape[1], INNER)
        return out @ Wo + bo

    def _L0_attn_ref(x, w_attn, w_proj):
        import jax, jax.numpy as jnp
        import numpy as np
        import math
        D = 256
        H = 16
        HEAD_D = D // H
        T = 512
        B = 4
        Bv, Tv, _ = x.shape
        qkv = x @ w_attn
        q = qkv[..., :D].reshape(Bv, Tv, H, HEAD_D).transpose(0, 2, 1, 3)
        k = qkv[..., D:D + HEAD_D]
        v = qkv[..., D + HEAD_D:]
        scale = 1.0 / math.sqrt(HEAD_D)
        att = jnp.einsum('bhqd,bkd->bhqk', q, k) * scale
        causal = jnp.tril(jnp.ones((Tv, Tv), dtype=bool))
        att = jnp.where(causal[None, None, :, :], att, -jnp.inf)
        att = jax.nn.softmax(att, axis=-1)
        y = jnp.einsum('bhqk,bkd->bhqd', att, v)
        y = y.transpose(0, 2, 1, 3).reshape(Bv, Tv, D)
        return y @ w_proj

    def _L0_ffn_ref(x, router_w, router_b, routed_w1, routed_w3, routed_w2, shared_w1, shared_w3, shared_w2):
        import jax, jax.numpy as jnp
        import numpy as np
        BEST_K = 2

        def _expert(xf, w1, w3, w2):
            return jax.nn.silu(xf @ w1) * (xf @ w3) @ w2
        B, S, D = x.shape
        T = B * S
        xf = x.reshape(T, D)
        logits = xf @ router_w + router_b
        topk_vals, topk_idx = jax.lax.top_k(logits, BEST_K)
        sparse = jnp.full_like(logits, -jnp.inf)
        sparse = sparse.at[jnp.arange(T)[:, None], topk_idx].set(topk_vals)
        gates = jax.nn.softmax(sparse, axis=-1)
        routed = jax.vmap(_expert, in_axes=(None, 0, 0, 0))(xf, routed_w1, routed_w3, routed_w2)
        routed_out = jnp.einsum('etd,te->td', routed, gates)
        shared_out = jax.vmap(_expert, in_axes=(None, 0, 0, 0))(xf, shared_w1, shared_w3, shared_w2).sum(axis=0)
        return (routed_out + shared_out).reshape(B, S, D)
    x = x + _L0_xattn_ref(_layernorm(x, axis=-1), ctx_768, L0_xattn_Wq, L0_xattn_Wk, L0_xattn_Wv, L0_xattn_Wo, L0_xattn_bo)
    x = x + _L0_attn_ref(_layernorm(x, axis=-1), L0_attn_w_attn, L0_attn_w_proj)
    x = x + _L0_ffn_ref(_layernorm(x, axis=-1), L0_ffn_router_w, L0_ffn_router_b, L0_ffn_routed_w1, L0_ffn_routed_w3, L0_ffn_routed_w2, L0_ffn_shared_w1, L0_ffn_shared_w3, L0_ffn_shared_w2)
    return x

_drawn_inputs = setup_inputs


def setup_inputs(seed=0):
    import zlib

    import numpy as np

    out = dict(_drawn_inputs(seed))
    spreads = {'L0_ffn_router_b': (0.0, 0.8)}
    factors = {'L0_xattn_bo': 5.72,
     'L0_ffn_router_w': 8.0,
     'L0_ffn_routed_w1': 8.0,
     'L0_ffn_routed_w3': 8.0,
     'L0_ffn_routed_w2': 8.0,
     'L0_ffn_shared_w1': 4.281,
     'L0_ffn_shared_w3': 4.189,
     'L0_ffn_shared_w2': 4.179}
    for name, (base, spread) in spreads.items():
        noise = np.random.default_rng([zlib.crc32(name.encode()), seed]).standard_normal(out[name].shape)
        drawn = base * np.exp(spread * noise) if base else spread * noise
        out[name] = jnp.asarray(drawn.astype(out[name].dtype))
    for name, factor in factors.items():
        out[name] = (out[name] * factor).astype(out[name].dtype)
    return out
```

```python
from contextlib import ExitStack

import concourse.bass as bass
import numpy as np
from concourse import mybir

F32 = mybir.dt.float32
F16 = mybir.dt.float16
BF16 = mybir.dt.bfloat16
U32 = mybir.dt.uint32
ALU = mybir.AluOpType
ACT = mybir.ActivationFunctionType
AX_X = mybir.AxisListType.X

P = 128
N = 256
NQ = N // P
D = 256
DC = D // P
M = 4096
CD = 192
HEADS = 16
HD = 64
PAIRS = HEADS // 2
TILES = M // P
CHUNK = 512
CHUNKS = M // CHUNK
GROUP = 4
GROUPS = TILES // GROUP
RESTACK = 1024
RESTACKS = M // RESTACK
PROBS = 8
W_SCALE = 256.0
MAX_UNIT = 64.0
Q_SCALE = float(HD) ** -0.5
EPS = 1e-5

SHD = 16
SH8 = P // SHD
S_SCALE = float(SHD) ** -0.5
MASKED = -1e30
E = 8
ES = 2
EA = E + ES
H = 128

HEAD = 8
Q_STEP = 8
K_STEP = 9
MAX_STEP = 11
V_STEP = 17
M4_STEP = 27
ROWS_STEP = 29
MAXES = 2 * NQ * CHUNKS
IDENT_CONSTS, ZERO_CONSTS, QK_CONSTS, ALL_CONSTS = 6, 8, 11, 17
MAX_UNITS = float(np.array([MAX_UNIT] * 2, np.float16).view(np.float32)[0])
LAST_ODD = (TILES - HEAD) // 2
A1, B1, A2, B2 = range(4)


def build(nc, x, ctx_main, ctx_tail, w_kv, w_q, w_o, bo, w_sq, w_sk, w_sv, w_proj, router_w,
          router_b, w1, w3, w2, out):
    with ExitStack() as stack:
        def sb(name, shape, dt):
            return stack.enter_context(nc.sbuf_tensor(name, shape, dt))

        def sem(name):
            return stack.enter_context(nc.semaphore(name))

        ctx_hi = sb("ctx_hi", [P, M], F16)
        ctx_lo = sb("ctx_lo", [P, M], F16)
        ctx_st = sb("ctx_st", [P, M], F16)
        ctx_raw = sb("ctx_raw", [P, 2, 2, RESTACK], F32)
        k_hi = sb("k_hi", [P, M], F16)
        k_lo = sb("k_lo", [P, M], F16)
        k_st = sb("k_st", [P, 4, M], F16)
        v = sb("v", [P, TILES, P], F32)
        probs = sb("probs", [P, PROBS, 2 * N], F32)
        prob_sums = sb("prob_sums", [P, 2 * N], F32)
        odd_sums = sb("odd_sums", [P, 2 * N], F32)
        kv_raw = sb("kv_raw", [P, 4 * P], F32)
        kv_hi = sb("kv_hi", [P, 4 * P], F16)
        kv_lo = sb("kv_lo", [P, 4 * P], F16)
        q_raw = sb("q_raw", [P, DC, P], F32)
        o_raw = sb("o_raw", [P, D], F32)
        q_nat = sb("q_nat", [P, 2, N], F16)
        q_st = sb("q_st", [P, 4, N], F16)
        max_part = sb("max_part", [P, 2 * NQ, CHUNKS], F32)
        max4 = sb("max4", [P, 2 * NQ], F32)
        neg_max = sb("neg_max", [P, 2 * NQ], F16)
        o_sum = sb("o_sum", [P, N], F32)
        inv_sum = sb("inv_sum", [P, N], F32)
        o_norm = sb("o_norm", [P, N], F32)
        ones = sb("ones", [P, P], F32)
        ident = sb("ident", [P, P], F32)
        ident_h = sb("ident_h", [P, P], F16)
        ident_b = sb("ident_b", [P, P], BF16)
        xs = sb("xs", [P, NQ, D], F32)
        x_in = sb("x_in", [P, NQ, D], F32)
        bo_all = sb("bo_all", [P, D], F32)
        xn = sb("xn", [P, NQ, D], F32)
        xt = sb("xt", [P, DC, N], F32)
        stats = sb("stats", [P, NQ, 6], F32)
        mean_var = sb("mean_var", [P, NQ, 2], F32)
        std = sb("std", [P, NQ], F32)
        inv_std = sb("inv_std", [P, NQ], F32)
        w_sq_sb = sb("w_sq_sb", [P, DC, D], F32)
        w_sk_sb = sb("w_sk_sb", [P, DC, P], F32)
        w_sv_sb = sb("w_sv_sb", [P, DC, SHD], F32)
        w_proj_sb = sb("w_proj_sb", [P, DC, D], F32)
        head_rows = sb("head_rows", [P, SH8], F32)
        diag4 = sb("diag4", [P, 4, P], BF16)
        sq = sb("sq", [P, DC, N], F32)
        sk_blocks = sb("sk_blocks", [P, SH8, N], F32)
        sv = sb("sv", [P, NQ, SHD + 1], F32)
        smax = sb("smax", [P, 12, 4], F32)
        sneg = sb("sneg", [P, 12, 4], F32)
        sinv = sb("sinv", [P, NQ, HEADS], F32)
        sy = sb("sy", [P, NQ, D], F32)
        sp = k_st[:, :, :].rearrange("p a m -> p (a m)").bitcast(F32).rearrange("p (f n) -> p f n", n=512)
        spt = v[:, :, :].rearrange("p t n -> p (t n)").rearrange("p (f n) -> p f n", n=512)
        yt = sb("yt", [P, DC, N], F32)
        router_w_sb = sb("router_w_sb", [P, DC, E], F32)
        router_b_sb = sb("router_b_sb", [P, E], F32)
        expert_no = sb("expert_no", [P, E], F32)
        logits = sb("logits", [P, NQ, E], F32)
        top8 = sb("top8", [P, NQ, 8], F32)
        top_at = sb("top_at", [P, NQ, 8], U32)
        top_no = sb("top_no", [P, NQ, 2], F32)
        gap = sb("gap", [P, NQ], F32)
        e_gap = sb("e_gap", [P, NQ], F32)
        e_gap1 = sb("e_gap1", [P, NQ], F32)
        gate12 = sb("gate12", [P, NQ, 2], F32)
        first_gate = sb("first_gate", [P, NQ, E], F32)
        second_gate = sb("second_gate", [P, NQ, E], F32)
        gates = sb("gates", [P, NQ, E], F32)
        w1_sb = sb("w1_sb", [P, EA, DC, H], F32)
        w3_sb = sb("w3_sb", [P, EA, DC, H], F32)
        w2_sb = ctx_raw[:, :, :, :].rearrange("p a b m -> p (a b m)")[:, 0:EA * D].rearrange(
            "p (e d) -> p e d", e=EA)
        act_h = sb("act_h", [P, 2, N], F32)
        gated = sb("gated", [P, EA, N], F32)

        bank = [stack.enter_context(nc.psum_tensor(f"bank{i}", [P, 512], F32)) for i in range(8)]
        score_b = bank[0:2]
        out_b = bank[2]
        kv_b = bank[3:5]
        max_b = bank[5:7]
        misc_b = bank[7]

        x_loaded, bo_loaded, w_tail_loaded = sem("x_loaded"), sem("bo_loaded"), sem("w_tail_loaded")
        w2_loaded = sem("w2_loaded")
        ctx_loaded = [sem(f"ctx_loaded{i}") for i in range(RESTACKS)]
        kv_loaded, q_loaded, o_loaded = sem("kv_loaded"), sem("q_loaded"), sem("o_loaded")
        restacked = [sem(f"restacked{i}") for i in range(RESTACKS)]
        ctx_hi_ready, ctx_lo_ready, ctx_pool_lo = sem("ctx_hi_ready"), sem("ctx_lo_ready"), sem("ctx_pool_lo")
        consts = sem("consts")
        w_split = sem("w_split")
        q_ready, q_taken = sem("q_ready"), sem("q_taken")
        kv_ready = sem("kv_ready")
        k_hi_ready, k_lo_ready, v_ready = sem("k_hi_ready"), sem("k_lo_ready"), sem("v_ready")
        max_ready, max_taken = sem("max_ready"), sem("max_taken")
        max4_ready, neg_max_ready = sem("max4_ready"), sem("neg_max_ready")
        rows_ready = sem("rows_ready")
        q_stacked = sem("q_stacked")
        scores_ready, probs_ready = sem("scores_ready"), sem("probs_ready")
        pv_done, summed = sem("pv_done"), sem("summed")
        summed_odd = sem("summed_odd")
        out_taken, sums_ready, inv_ready = sem("out_taken"), sem("sums_ready"), sem("inv_ready")
        o_norm_ready, wo_ready, x_added = sem("o_norm_ready"), sem("wo_ready"), sem("x_added")
        var_ready, std_ready, xn_ready = sem("var_ready"), sem("std_ready"), sem("xn_ready")
        xt_psum, xt_ready = sem("xt_psum"), sem("xt_ready")
        sproj_ready, sproj_taken, sq_taken = sem("sproj_ready"), sem("sproj_taken"), sem("sq_taken")
        s_scores, s_neg, s_exp = sem("s_scores"), sem("s_neg"), sem("s_exp")
        s_pt, s_pt_taken, s_pv = sem("s_pt"), sem("s_pt_taken"), sem("s_pv")
        sy_ready, yt_psum, yt_ready, sproj_out = sem("sy_ready"), sem("yt_psum"), sem("yt_ready"), sem("sproj_out")
        router_ready, gap_ready, gap_exp = sem("router_ready"), sem("gap_ready"), sem("gap_exp")
        h_ready, silu_ready, gated_ready = sem("h_ready"), sem("silu_ready"), sem("gated_ready")
        expert_out, expert_added = sem("expert_out"), sem("expert_added")
        dve_step = sem("dve_step")
        stored = sem("stored")

        block = stack.enter_context(nc.Block())

        def raw_chunk(j):
            if j < 2:
                return ctx_raw[:, j, 0, :], ctx_raw[:, j, 1, :]
            t = (j - 2) * (TILES // 2)
            return (v[:, tokens(t, TILES // 4), :].rearrange("p t n -> p (t n)"),
                    v[:, tokens(t + TILES // 4, TILES // 4), :].rearrange("p t n -> p (t n)"))

        def wait_ctx_split(engine, j):
            engine.wait_ge(ctx_hi_ready, 2 * (j + 1))
            engine.wait_ge(ctx_lo_ready, min(j + 1, 2))
            engine.wait_ge(ctx_pool_lo, j + 1 if j < 2 else 2 * j)

        def tokens(first, count):
            return slice(first, first + count)

        def fill_shape(f):
            return (4, P) if f % 6 < 2 else (2, 2 * P)

        def spt_of(f):
            if f < 8:
                return spt[:, f, :]
            part = (k_hi, k_lo)[(f - 8) // 2][:, :].bitcast(F32)
            return part[:, ((f - 8) % 2) * 512:((f - 8) % 2 + 1) * 512]

        def repeated(ap, n):
            return ap.rearrange("p (a m) -> p a m", a=1).broadcast_to([ap.shape[0], n, ap.shape[1]])

        @block.sync
        def _(sp_q):
            sp_q.dma_start(x_in[:, :, :], x.rearrange("(h p) d -> p h d", p=P)).then_inc(x_loaded, 16)
            sp_q.dma_start(kv_raw[:, :], w_kv[0]).then_inc(kv_loaded, 16)
            sp_q.dma_start(q_raw[:, :, :], w_q[0]).then_inc(q_loaded, 16)

            def load_ctx(j):
                sl = tokens(RESTACK * j, RESTACK)
                main, tail = raw_chunk(j)
                sp_q.dma_start(main, ctx_main[:, sl]).then_inc(ctx_loaded[j], 16)
                sp_q.dma_start(tail[0:HD, :], ctx_tail[:, sl]).then_inc(ctx_loaded[j], 16)
                sp_q.dma_start(tail[HD:P, :], ctx_tail[:, sl]).then_inc(ctx_loaded[j], 16)

            load_ctx(0)
            load_ctx(1)
            sp_q.dma_start(bo_all[:, :], bo.rearrange("(a d) -> a d", a=1).broadcast_to([P, D])).then_inc(bo_loaded, 16)
            load_ctx(2)
            load_ctx(3)
            sp_q.wait_ge(w_split, 2)
            sp_q.dma_start(kv_raw[:, :], w_kv[1]).then_inc(kv_loaded, 16)
            sp_q.wait_ge(q_ready, 1)
            sp_q.dma_start(q_raw[:, :, :], w_q[1]).then_inc(q_loaded, 16)

            def restack(g, parts, former_scores=None):
                sp_q.wait_ge(k_lo_ready, parts)
                sp_q.wait_ge(k_hi_ready, parts)
                if former_scores is not None:
                    sp_q.wait_ge(scores_ready, former_scores)
                sl = tokens(RESTACK * g, RESTACK)
                for rows, to, which, part in (
                    (slice(0, HD), slice(0, HD), A1, k_hi), (slice(0, HD), slice(0, HD), A2, k_hi),
                    (slice(HD, P), slice(HD, P), B1, k_hi), (slice(HD, P), slice(HD, P), B2, k_hi),
                    (slice(0, HD), slice(HD, P), A1, k_lo), (slice(HD, P), slice(0, HD), B1, k_lo),
                ):
                    sp_q.dma_start(k_st[to, which, sl], part[rows, sl]).then_inc(restacked[g], 16)

            sp_q.wait_ge(consts, ZERO_CONSTS)
            for g in range(RESTACKS):
                restack(g, 2 * (g + 1))
            for to, frm in (
                (w_sq_sb[:, :, :], w_sq.rearrange("(c p) n -> p c n", p=P)),
                (w_sk_sb[:, :, :], w_sk.rearrange("(c p) n -> p c n", p=P)),
                (w_sv_sb[:, :, :], w_sv.rearrange("(c p) n -> p c n", p=P)),
                (w_proj_sb[:, :, :], w_proj.rearrange("(c p) n -> p c n", p=P)),
                (router_w_sb[:, :, :], router_w.rearrange("(c p) n -> p c n", p=P)),
                (router_b_sb[:, :], router_b.rearrange("(a d) -> a d", a=1).broadcast_to([P, E])),
                (w1_sb[:, :, :, :], w1.rearrange("e (c p) h -> p e c h", p=P)),
                (w3_sb[:, :, :, :], w3.rearrange("e (c p) h -> p e c h", p=P)),
            ):
                sp_q.dma_start(to, frm).then_inc(w_tail_loaded, 16)
            wait_ctx_split(sp_q, 1)
            sp_q.dma_start(w2_sb, w2.rearrange("e h d -> h e d")).then_inc(w2_loaded, 16)

            with sp_q.Fori(0, PAIRS - 1) as i:
                def now(value):
                    return sp_q.snap(sp_q.to_reg(value))

                after_next = now(i + 2)
                split = now(i * 2 + 4)
                parts = [now((i + 1) * CHUNKS + 2 * (g + 1)) for g in range(RESTACKS)]
                former = [now(i * TILES + 8 * (g + 1)) for g in range(RESTACKS)]
                w_o_i = w_o[bass.ds(i, 1), :, :].rearrange("a p d -> (a p) d")
                w_kv_i = w_kv[bass.ds(after_next, 1), :, :].rearrange("a p d -> (a p) d")
                w_q_i = w_q[bass.ds(after_next, 1), :, :, :].rearrange("a p c d -> (a p) c d")
                sp_q.wait_ge(x_added, i + 1)
                sp_q.dma_start(o_raw[:, :], w_o_i).then_inc(o_loaded, 16)
                sp_q.wait_ge(w_split, split)
                sp_q.dma_start(kv_raw[:, :], w_kv_i).then_inc(kv_loaded, 16)
                sp_q.wait_ge(q_ready, after_next)
                sp_q.dma_start(q_raw[:, :, :], w_q_i).then_inc(q_loaded, 16)
                for g in range(RESTACKS):
                    restack(g, parts[g], former[g])
            sp_q.wait_ge(wo_ready, PAIRS - 1)
            sp_q.dma_start(o_raw[:, :], w_o[PAIRS - 1]).then_inc(o_loaded, 16)
            sp_q.wait_ge(kv_loaded, 16 * (PAIRS + 1))
            sp_q.wait_ge(q_loaded, 16 * (PAIRS + 1))

            sp_q.wait_ge(expert_added, EA)
            sp_q.dma_start(out.rearrange("(h p) d -> p h d", p=P), xs[:, :, :]).then_inc(stored, 16)
            sp_q.wait_ge(stored, 16)

        @block.gpsimd
        def _(pool):
            made = [0]

            def const(ins):
                made[0] += 1
                ins.then_inc(consts, 1)
                pool.wait_ge(consts, made[0])

            for m in (ident, ident_h, ident_b):
                const(pool.memset(m[:, :], 0.0))
                const(pool.affine_select(out=m[:, :], in_=m[:, :], compare_op=ALU.not_equal, fill=1.0, base=0,
                                         pattern=[[-1, P]], channel_multiplier=1))
            const(pool.memset(k_st[:, A2:B2 + 1, :].rearrange("p a m -> p (a m)").bitcast(F32), 0.0))
            const(pool.memset(q_st[:, A2:B2 + 1, :], 0.0))
            split = 0
            for j in range(RESTACKS):
                sl = tokens(RESTACK * j, RESTACK)
                main, tail = raw_chunk(j)
                pool.wait_ge(ctx_loaded[j], 48)
                if j >= 2:
                    pool.wait_ge(ctx_hi_ready, 2 * j + 1)
                    pool.tensor_tensor(ctx_lo[:, sl], main, ctx_hi[:, sl], ALU.subtract).then_inc(ctx_pool_lo, 1)
                    split += 1
                    pool.wait_ge(ctx_pool_lo, split)
                pool.wait_ge(ctx_hi_ready, 2 * j + 2)
                pool.tensor_tensor(ctx_st[HD:P, sl], tail[HD:P, :], ctx_st[HD:P, sl],
                                   ALU.subtract).then_inc(ctx_pool_lo, 1)
                split += 1
                pool.wait_ge(ctx_pool_lo, split)
            const(pool.memset(k_st[HD:HD + 1, A2, :].bitcast(F32), MAX_UNITS))
            const(pool.memset(k_st[0:1, B2, :].bitcast(F32), MAX_UNITS))
            const(pool.memset(ones[:, :], 1.0))
            const(pool.memset(diag4[:, :, :], 0.0))
            const(pool.affine_select(out=diag4[:, :, :], in_=diag4[:, :, :], compare_op=ALU.is_ge,
                                     fill=MASKED, base=0, pattern=[[0, 4], [-1, P]], channel_multiplier=1))
            const(pool.memset(head_rows[:, :], 1.0))
            const(pool.affine_select(out=head_rows[:, :], in_=head_rows[:, :], compare_op=ALU.is_ge,
                                     fill=0.0, base=0, pattern=[[-SHD, SH8]], channel_multiplier=1))
            const(pool.affine_select(out=head_rows[:, :], in_=head_rows[:, :], compare_op=ALU.is_ge,
                                     fill=0.0, base=SHD - 1, pattern=[[SHD, SH8]], channel_multiplier=-1))
            const(pool.iota(expert_no[:, :], pattern=[[1, E]], base=0, channel_multiplier=0,
                            allow_small_or_imprecise_dtypes=True))

            def step(p, t, first=False):
                if t == 0:
                    return
                pool.wait_ge(probs_ready, p * TILES + t + 1)
                if t == 1:
                    if not first:
                        pool.wait_ge(sums_ready, p)
                    pool.tensor_tensor(prob_sums[:, :], probs[:, 0, :], probs[:, 1, :], ALU.add).then_inc(summed, 2)
                else:
                    pool.wait_ge(summed, p * TILES + t)
                    pool.tensor_tensor(prob_sums[:, :], prob_sums[:, :], probs[:, t % PROBS, :], ALU.add).then_inc(summed, 1)

            for t in range(HEAD):
                step(0, t, True)
            with pool.Fori(0, PAIRS - 1) as i:
                for t in range(HEAD, TILES):
                    step(i, t)
                for t in range(HEAD):
                    step(i + 1, t)
            for t in range(HEAD, TILES, 2):
                pool.wait_ge(probs_ready, (PAIRS - 1) * TILES + t + 1)
                pool.wait_ge(summed, (PAIRS - 1) * TILES + HEAD + (t - HEAD) // 2)
                pool.tensor_tensor(prob_sums[:, :], prob_sums[:, :], probs[:, t % PROBS, :], ALU.add).then_inc(summed, 1)

        @block.scalar
        def _(act):
            def sqrt_var(k):
                act.wait_ge(var_ready, k)
                act.activation(std[:, :], mean_var[:, :, 1], ACT.Sqrt).then_inc(std_ready, 1)

            sqrt_var(1)

            def split_ctx(j):
                act.wait_ge(ctx_loaded[j], 48)
                sl = tokens(RESTACK * j, RESTACK)
                main, tail = raw_chunk(j)
                act.copy(ctx_hi[:, sl], main).then_inc(ctx_hi_ready, 1)
                act.copy(ctx_st[:, sl], tail).then_inc(ctx_hi_ready, 1)

            def step(p, t, first=False, last=False):
                act.wait_ge(scores_ready, p * TILES + t + 1)
                if not first:
                    former = t - PROBS
                    act.wait_ge(pv_done, p * TILES + former + 1)
                    if not last or former < HEAD:
                        act.wait_ge(summed, p * TILES + former + 1)
                    elif former % 2 == 0:
                        act.wait_ge(summed, p * TILES + HEAD + (former - HEAD) // 2 + 1)
                    else:
                        act.wait_ge(summed_odd, (former - HEAD) // 2 + 1)
                act.activation(probs[:, t % PROBS, :], score_b[t % 2][:, :], ACT.Exp).then_inc(probs_ready, 1)

            def prepare(n, t, former=True):
                if K_STEP <= t < K_STEP + CHUNKS:
                    c = t - K_STEP
                    act.wait_ge(kv_ready, n * (CHUNKS + GROUPS) + c + 1)
                    if former:
                        act.wait_ge(restacked[c // 2], n * 96)
                        act.wait_ge(max_ready, n * MAXES)
                    act.activation(k_hi[:, tokens(CHUNK * c, CHUNK)], kv_b[c % 2][:, :], ACT.Copy,
                                   scale=1.0 / W_SCALE).then_inc(k_hi_ready, 1)
                if V_STEP <= t < V_STEP + 2 * (GROUPS - 2) and (t - V_STEP) % 2 == 0:
                    values(n, (t - V_STEP) // 2, former)

            def values(n, g, former=True):
                act.wait_ge(kv_ready, n * (CHUNKS + GROUPS) + CHUNKS + g + 1)
                if former:
                    act.wait_ge(pv_done, (n - 1) * TILES + GROUP * (g + 1))
                elif g == 0:
                    wait_ctx_split(act, RESTACKS - 1)
                act.activation(v[:, tokens(GROUP * g, GROUP), :].rearrange("p t n -> p (t n)"),
                               kv_b[g % 2][:, :], ACT.Copy, scale=1.0 / W_SCALE).then_inc(v_ready, 1)

            split_ctx(0)
            split_ctx(1)
            for t in range(HEAD, TILES):
                if t in (K_STEP, K_STEP + 2):
                    split_ctx((t - K_STEP) // 2 + 2)
                prepare(0, t, False)
            values(0, GROUPS - 2, False)
            values(0, GROUPS - 1, False)
            for t in range(HEAD):
                step(0, t, True)
            with act.Fori(0, PAIRS - 1) as i:
                for t in range(HEAD, TILES):
                    step(i, t)
                    prepare(i + 1, t)
                values(i + 1, GROUPS - 2)
                for t in range(HEAD):
                    step(i + 1, t)
                    if t == 1:
                        values(i + 1, GROUPS - 1)
            for t in range(HEAD, TILES):
                step(PAIRS - 1, t, last=True)

            sqrt_var(2)
            act.wait_ge(sproj_ready, 2)
            act.activation(sq[:, :, :].rearrange("p c n -> p (c n)"), kv_b[1][:, :], ACT.Copy,
                           scale=S_SCALE).then_inc(sq_taken, 1)
            for f in range(12):
                heads, keys = fill_shape(f)
                act.wait_ge(s_neg, f + 1)
                for h in range(heads):
                    last = act.activation(sp[:, f, h * keys:(h + 1) * keys],
                                          bank[f % 3][:, h * keys:(h + 1) * keys], ACT.Exp,
                                          bias=sneg[:, f, h:h + 1])
                last.then_inc(s_exp, 1)
            sqrt_var(3)
            act.wait_ge(gap_ready, 1)
            act.activation(e_gap[:, :], gap[:, :], ACT.Exp).then_inc(gap_exp, 1)
            for e in range(EA):
                act.wait_ge(h_ready, e + 1)
                if e >= 2:
                    act.wait_ge(gated_ready, e - 1)
                act.activation(act_h[:, e % 2, :], bank[e % 3][:, 0:N], ACT.Silu).then_inc(silu_ready, 1)

        @block.vector
        def _(dve):
            chain = [0]

            def link(ins):
                chain[0] += 1
                ins.then_inc(dve_step, 1)
                dve.wait_ge(dve_step, chain[0])

            def layernorm(src, k):
                for h in range(NQ):
                    link(dve.bn_stats(stats[:, h, :], src[:, h, :]))
                    link(dve.bn_aggr(mean_var[:, h, :], stats[:, h, :]))
                dve.tensor_scalar(mean_var[:, :, 1], mean_var[:, :, 1], EPS, None, ALU.add).then_inc(var_ready, 1)
                dve.wait_ge(std_ready, k)
                link(dve.reciprocal(inv_std[:, :], std[:, :]))
                for h in range(NQ):
                    dve.tensor_scalar(xn[:, h, :], src[:, h, :], mean_var[:, h, 0:1], inv_std[:, h:h + 1],
                                      ALU.subtract, ALU.mult).then_inc(xn_ready, 1)

            def transposed(src_bank, k):
                dve.wait_ge(xt_psum, k)
                dve.tensor_copy(xt[:, :, :].rearrange("p c n -> p (c n)"), src_bank[:, :]).then_inc(xt_ready, 1)

            dve.wait_ge(x_loaded, 16)
            layernorm(x_in, 1)
            transposed(out_b, 1)

            def split_ctx(j):
                sl = tokens(RESTACK * j, RESTACK)
                dve.wait_ge(ctx_loaded[j], 48)
                dve.wait_ge(ctx_hi_ready, 2 * j + 1)
                dve.tensor_tensor(ctx_lo[:, sl], raw_chunk(j)[0], ctx_hi[:, sl], ALU.subtract).then_inc(ctx_lo_ready, 1)

            def split_weights(n, former=True):
                dve.wait_ge(kv_loaded, n * 16 + 16)
                if former:
                    dve.wait_ge(v_ready, n * GROUPS)
                dve.tensor_scalar(kv_hi[:, :], kv_raw[:, :], W_SCALE, None, ALU.mult).then_inc(w_split, 1)
                dve.wait_ge(w_split, n * 2 + 1)
                dve.scalar_tensor_tensor(kv_lo[:, :], kv_raw[:, :], W_SCALE, kv_hi[:, :],
                                         ALU.mult, ALU.subtract).then_inc(w_split, 1)

            def split_queries(n, former=True):
                dve.wait_ge(q_ready, n + 1)
                if former:
                    dve.wait_ge(max_ready, n * MAXES)
                    dve.wait_ge(q_stacked, n * 6)
                dve.tensor_scalar(q_nat[:, 0, :], misc_b[:, 0:N], Q_SCALE, None, ALU.mult).then_inc(q_taken, 1)
                dve.wait_ge(q_taken, n * 2 + 1)
                dve.scalar_tensor_tensor(q_nat[:, 1, :], misc_b[:, 0:N], Q_SCALE, q_nat[:, 0, :],
                                         ALU.mult, ALU.subtract).then_inc(q_taken, 1)

            def prepare(n, t, former=True):
                if t == Q_STEP:
                    split_weights(n, former)
                    split_queries(n, former)
                def part_max(j):
                    dve.wait_ge(max_ready, n * MAXES + j + 1)
                    if former and j == 0:
                        dve.wait_ge(max4_ready, n)
                    dve.tensor_reduce(max_part[:, j % 4, j // 4:j // 4 + 1], max_b[j % 2][:, :], AX_X,
                                      ALU.max).then_inc(max_taken, 1)

                maxes = MAX_STEP <= t < MAX_STEP + MAXES // 2
                if maxes:
                    part_max(2 * (t - MAX_STEP))
                if K_STEP <= t < K_STEP + CHUNKS:
                    c = t - K_STEP
                    sl = tokens(CHUNK * c, CHUNK)
                    dve.wait_ge(k_hi_ready, n * CHUNKS + c + 1)
                    if former:
                        dve.wait_ge(restacked[c // 2], n * 96)
                    dve.scalar_tensor_tensor(k_lo[:, sl], kv_b[c % 2][:, :], 1.0 / W_SCALE, k_hi[:, sl],
                                             ALU.mult, ALU.subtract).then_inc(k_lo_ready, 1)
                if maxes:
                    part_max(2 * (t - MAX_STEP) + 1)
                if t == M4_STEP:
                    dve.wait_ge(max_taken, n * MAXES + MAXES)
                    if former:
                        dve.wait_ge(neg_max_ready, n)
                        dve.wait_ge(rows_ready, n)
                    dve.tensor_reduce(max4[:, :], max_part[:, :, :], AX_X, ALU.max).then_inc(max4_ready, 1)
                    dve.wait_ge(max4_ready, n + 1)
                    dve.tensor_scalar(neg_max[:, :], max4[:, :], -1.0 / MAX_UNIT, None, ALU.mult).then_inc(neg_max_ready, 1)

            def stack_queries(n, former=True):
                if former:
                    dve.wait_ge(scores_ready, n * TILES)
                dve.wait_ge(q_taken, n * 2 + 2)
                dve.tensor_copy(q_st[0:HD, A1:B2 + 1:2, :], q_nat[0:HD, :, :]).then_inc(q_stacked, 1)
                dve.tensor_copy(q_st[HD:P, B1:B2 + 1:2, :], q_nat[HD:P, :, :]).then_inc(q_stacked, 1)
                dve.tensor_copy(q_st[HD:P, A1, :], q_nat[0:HD, 0, :]).then_inc(q_stacked, 1)
                dve.tensor_copy(q_st[0:HD, B1, :], q_nat[HD:P, 0, :]).then_inc(q_stacked, 1)
                dve.wait_ge(rows_ready, n + 1)
                dve.tensor_copy(q_st[HD:HD + 1, A2, :], misc_b[HD:HD + 1, 0:N]).then_inc(q_stacked, 1)
                dve.tensor_copy(q_st[0:1, B2, :], misc_b[0:1, 0:N]).then_inc(q_stacked, 1)

            def take_output(p):
                dve.wait_ge(pv_done, p * TILES + TILES)
                dve.wait_ge(x_added, p + 1)
                dve.tensor_copy(o_sum[:, :], out_b[:, 0:N]).then_inc(out_taken, 1)

            def normalise(p):
                dve.wait_ge(sums_ready, p)
                dve.reciprocal(inv_sum[:, :], misc_b[:, 0:N]).then_inc(inv_ready, 1)
                dve.wait_ge(inv_ready, p)
                dve.wait_ge(out_taken, p)
                dve.wait_ge(x_added, p)
                dve.tensor_tensor(o_norm[:, :], o_sum[:, :], inv_sum[:, :], ALU.mult).then_inc(o_norm_ready, 1)

            def add_output(p):
                dve.wait_ge(wo_ready, p)
                dve.wait_ge(x_added, p)
                dve.tensor_tensor(xs[:, :, :].rearrange("p h d -> p (h d)"), misc_b[:, :],
                                  xs[:, :, :].rearrange("p h d -> p (h d)"), ALU.add).then_inc(x_added, 1)

            def finish(p, t):
                if t == 2:
                    normalise(p)
                if t == 5:
                    add_output(p)

            split_weights(0, False)
            split_ctx(0)
            split_queries(0, False)
            for t in range(K_STEP, TILES):
                if t == K_STEP + 2:
                    split_ctx(1)
                prepare(0, t, False)
            dve.wait_ge(bo_loaded, 16)
            for h in range(NQ):
                ins = dve.tensor_tensor(xs[:, h, :], x_in[:, h, :], bo_all[:, :], ALU.add)
            ins.then_inc(x_added, 1)
            dve.wait_ge(consts, QK_CONSTS)
            stack_queries(0, False)
            with dve.Fori(0, PAIRS - 1) as i:
                for t in range(HEAD, TILES):
                    prepare(i + 1, t)
                stack_queries(i + 1)
                take_output(i)
                for t in range(HEAD):
                    finish(i + 1, t)
            for t in range(HEAD + 3, TILES, 2):
                dve.wait_ge(probs_ready, (PAIRS - 1) * TILES + t + 1)
                if t == HEAD + 3:
                    dve.tensor_tensor(odd_sums[:, :], probs[:, (t - 2) % PROBS, :], probs[:, t % PROBS, :],
                                      ALU.add).then_inc(summed_odd, 2)
                else:
                    dve.wait_ge(summed_odd, (t - HEAD) // 2)
                    dve.tensor_tensor(odd_sums[:, :], odd_sums[:, :], probs[:, t % PROBS, :],
                                      ALU.add).then_inc(summed_odd, 1)
            take_output(PAIRS - 1)
            normalise(PAIRS)
            add_output(PAIRS)
            dve.wait_ge(x_added, PAIRS + 1)

            layernorm(xs, 2)
            transposed(kv_b[0], 2)
            dve.wait_ge(sproj_ready, 1)
            dve.wait_ge(consts, ALL_CONSTS)
            dve.tensor_tensor(sk_blocks[:, :, :], repeated(max_b[0][:, 0:N], SH8),
                              head_rows[:, :].rearrange("p (h a) -> p h a", a=1).broadcast_to([P, SH8, N]),
                              ALU.mult).then_inc(sproj_taken, 1)
            dve.memset(sv[:, :, SHD:SHD + 1], 1.0).then_inc(sproj_taken, 1)
            dve.wait_ge(sproj_ready, 3)
            dve.tensor_copy(sv[:, :, 0:SHD], max_b[1][:, 0:NQ * SHD].rearrange("p (h n) -> p h n", h=NQ)).then_inc(sproj_taken, 1)

            def negative_maxima(f):
                heads, keys = fill_shape(f)
                dve.wait_ge(s_scores, f + 1)
                link(dve.tensor_reduce(smax[:, f, 0:heads], bank[f % 3][:, :].rearrange("p (h k) -> p h k", h=heads),
                                       AX_X, ALU.max))
                dve.tensor_scalar(sneg[:, f, 0:heads], smax[:, f, 0:heads], -1.0, None, ALU.mult).then_inc(s_neg, 1)

            def take_transposes(f):
                dve.wait_ge(s_pt, f + 1)
                dve.tensor_copy(spt_of(f), bank[3 + f % 2][:, :]).then_inc(s_pt_taken, 1)

            for f in range(12 + 2):
                if f < 12:
                    negative_maxima(f)
                if f >= 2:
                    take_transposes(f - 2)
            dve.wait_ge(s_pv, 12)
            for h in range(NQ):
                o = bank[6 + h][:, 0:HEADS * (SHD + 1)].rearrange("p (g n) -> p g n", n=SHD + 1)
                link(dve.reciprocal(sinv[:, h, :], o[:, :, SHD]))
                dve.tensor_tensor(sy[:, h, :].rearrange("p (g n) -> p g n", n=SHD), o[:, :, 0:SHD],
                                  sinv[:, h, :].rearrange("p (g a) -> p g a", a=1).broadcast_to([P, HEADS, SHD]),
                                  ALU.mult).then_inc(sy_ready, 1)
            dve.wait_ge(yt_psum, 1)
            dve.tensor_copy(yt[:, :, :].rearrange("p c n -> p (c n)"), bank[0][:, :]).then_inc(yt_ready, 1)
            dve.wait_ge(sproj_out, 1)
            link(dve.tensor_tensor(xs[:, :, :].rearrange("p h d -> p (h d)"), bank[1][:, :],
                                   xs[:, :, :].rearrange("p h d -> p (h d)"), ALU.add))

            layernorm(xs, 3)
            transposed(bank[2], 3)
            dve.wait_ge(router_ready, 1)
            for h in range(NQ):
                link(dve.tensor_tensor(logits[:, h, :], bank[3][:, h * E:(h + 1) * E], router_b_sb[:, :], ALU.add))
                link(dve.max(top8[:, h, :], logits[:, h, :]))
                link(dve.max_index(top_at[:, h, :], top8[:, h, :], logits[:, h, :]))
            link(dve.tensor_copy(top_no[:, :, :], top_at[:, :, 0:2]))
            dve.tensor_tensor(gap[:, :], top8[:, :, 1], top8[:, :, 0], ALU.subtract).then_inc(gap_ready, 1)
            dve.wait_ge(gap_exp, 1)
            link(dve.tensor_scalar(e_gap1[:, :], e_gap[:, :], 1.0, None, ALU.add))
            link(dve.reciprocal(gate12[:, :, 0], e_gap1[:, :]))
            link(dve.tensor_tensor(gate12[:, :, 1], gate12[:, :, 0], e_gap[:, :], ALU.mult))
            for h in range(NQ):
                link(dve.tensor_scalar(first_gate[:, h, :], expert_no[:, :], top_no[:, h, 0:1], gate12[:, h, 0:1],
                                       ALU.is_equal, ALU.mult))
                link(dve.tensor_scalar(second_gate[:, h, :], expert_no[:, :], top_no[:, h, 1:2], gate12[:, h, 1:2],
                                       ALU.is_equal, ALU.mult))
                link(dve.tensor_tensor(gates[:, h, :], first_gate[:, h, :], second_gate[:, h, :], ALU.add))

            def gate_up(e):
                dve.wait_ge(silu_ready, e + 1)
                dve.tensor_tensor(gated[:, e, :], bank[e % 3][:, N:2 * N], act_h[:, e % 2, :], ALU.mult).then_inc(gated_ready, 1)

            def add_expert(e):
                dve.wait_ge(expert_out, e + 1)
                for h in range(NQ):
                    o = bank[3 + e % 2][:, h * D:(h + 1) * D]
                    if e < E:
                        ins = dve.scalar_tensor_tensor(xs[:, h, :], o, gates[:, h, e:e + 1], xs[:, h, :], ALU.mult, ALU.add)
                    else:
                        ins = dve.tensor_tensor(xs[:, h, :], o, xs[:, h, :], ALU.add)
                ins.then_inc(expert_added, 1)
                dve.wait_ge(expert_added, e + 1)

            for e in range(EA + 1):
                if e < EA:
                    gate_up(e)
                if e >= 1:
                    add_expert(e - 1)
            

        @block.tensor
        def _(pe):
            def transposes(to, src, ready, count, done):
                pe.wait_ge(ready, count)
                for c in range(DC):
                    for h in range(NQ):
                        ins = pe.transpose(to[:, c * N + h * P:c * N + (h + 1) * P], src[:, h, c * P:(c + 1) * P], ident[:, :])
                ins.then_inc(done, 1)

            pe.wait_ge(consts, IDENT_CONSTS)
            transposes(out_b, xn, xn_ready, 2, xt_psum)

            def queries(n, former=True):
                pe.wait_ge(q_loaded, n * 16 + 16)
                if former:
                    pe.wait_ge(x_added, n)
                else:
                    pe.wait_ge(xt_ready, 1)
                for c in range(DC):
                    ins = pe.matmul(misc_b[:, 0:N], q_raw[:, c, :], xt[:, c, :], start=(c == 0), stop=(c == DC - 1))
                ins.then_inc(q_ready, 1)

            def five(main, tail):
                return ((kv_hi, main, ctx_hi), (kv_hi, main, ctx_lo), (kv_lo, main, ctx_hi),
                        (kv_hi, tail, ctx_st), (kv_lo, tail, ctx_st))

            def keys(n, c, former=True):
                if c == 0:
                    pe.wait_ge(w_split, n * 2 + 2)
                if not former:
                    wait_ctx_split(pe, c // 2)
                if c >= 2:
                    pe.wait_ge(k_lo_ready, n * CHUNKS + c - 1)
                elif former:
                    pe.wait_ge(v_ready, n * GROUPS - 1 + c)
                for s, (w, at, data) in enumerate(five(0, P)):
                    ins = pe.matmul(kv_b[c % 2][:, :], w[:, at:at + P], data[:, tokens(CHUNK * c, CHUNK)],
                                    start=(s == 0), stop=(s == 4))
                ins.then_inc(kv_ready, 1)

            def values(n, g):
                if g < 2:
                    pe.wait_ge(k_lo_ready, n * CHUNKS + CHUNKS - 1 + g)
                else:
                    pe.wait_ge(v_ready, n * GROUPS + g - 1)
                for j in range(GROUP):
                    for s, (w, at, data) in enumerate(five(2 * P, 3 * P)):
                        ins = pe.matmul(kv_b[g % 2][:, j * P:(j + 1) * P], data[:, tokens(P * (GROUP * g + j), P)],
                                        w[:, at:at + P], start=(s == 0), stop=(s == 4))
                ins.then_inc(kv_ready, 1)

            def max_scores(n, j, former=True):
                h, a, c = j % 2, (j // 2) % 2, j // 4
                if a == 0 and h == 0:
                    pe.wait_ge(k_hi_ready, n * CHUNKS + c + 1)
                if j == 0:
                    pe.wait_ge(q_taken, n * 2 + 1)
                if j >= 2 or former:
                    pe.wait_ge(max_taken, n * MAXES + j - 1)
                r = slice(HD * a, HD * a + HD)
                pe.matmul(max_b[j % 2][:, :], q_nat[r, 0, h * P:(h + 1) * P], k_hi[r, tokens(CHUNK * c, CHUNK)],
                          start=True, stop=True).then_inc(max_ready, 1)

            def max_rows(n):
                pe.wait_ge(neg_max_ready, n + 1)
                pe.wait_ge(q_taken, n * 2 + 2)
                for a, row in ((0, HD), (1, 0)):
                    for h in range(NQ):
                        ins = pe.matmul(misc_b[row:row + 1, h * P:(h + 1) * P], neg_max[:, a * 2 + h:a * 2 + h + 1],
                                        ident_h[:, :], start=True, stop=True)
                ins.then_inc(rows_ready, 1)

            def prepare(n, t, weigh_former=None):
                former = weigh_former is not None
                maxes = MAX_STEP <= t < MAX_STEP + MAXES // 2
                if t == Q_STEP:
                    queries(n, former)
                if maxes:
                    max_scores(n, 2 * (t - MAX_STEP), former)
                if K_STEP <= t < K_STEP + CHUNKS:
                    keys(n, t - K_STEP, former)
                if V_STEP <= t < V_STEP + 2 * (GROUPS - 2) and (t - V_STEP) % 2 == 0:
                    values(n, (t - V_STEP) // 2)
                if former:
                    weigh_former()
                if maxes:
                    max_scores(n, 2 * (t - MAX_STEP) + 1, former)
                if t == ROWS_STEP:
                    max_rows(n)

            def scores(p, t, first=False):
                if not first or t >= 2:
                    pe.wait_ge(probs_ready, p * TILES + t - 1)
                if t % 8 == 0:
                    pe.wait_ge(restacked[t // 8], p * 96 + 96)
                if t == 0:
                    pe.wait_ge(q_stacked, p * 6 + 6)
                sl = tokens(P * t, P)
                for k, (one, two) in enumerate(((A1, A2), (B1, B2))):
                    o = score_b[t % 2][:, k * N:(k + 1) * N]
                    pe.matmul(o, k_st[:, one, sl], q_st[:, one, :], start=True, stop=False)
                    ins = pe.matmul(o, k_st[:, two, sl], q_st[:, two, :], start=False, stop=True)
                ins.then_inc(scores_ready, 1)

            def weigh(p, t, first=False):
                pe.wait_ge(probs_ready, p * TILES + t + 1)
                if t % GROUP == 0:
                    pe.wait_ge(v_ready, p * GROUPS + t // GROUP + 1)
                if t == 0:
                    if not first:
                        pe.wait_ge(out_taken, p)
                for k in range(2):
                    ins = pe.matmul(out_b[HD * k:HD * (k + 1), 0:N], v[:, t, HD * k:HD * (k + 1)],
                                    probs[:, t % PROBS, k * N:(k + 1) * N], start=(t == 0), stop=(t == TILES - 1))
                ins.then_inc(pv_done, 1)

            def sums(p, last=False):
                pe.wait_ge(summed, p * TILES - (LAST_ODD if last else 0))
                if last:
                    pe.wait_ge(summed_odd, LAST_ODD)
                for k in range(2):
                    o = misc_b[HD * k:HD * (k + 1), 0:N]
                    ins = pe.matmul(o, ones[:, 0:HD], prob_sums[:, k * N:(k + 1) * N], start=True, stop=not last)
                    if last:
                        ins = pe.matmul(o, ones[:, 0:HD], odd_sums[:, k * N:(k + 1) * N], start=False, stop=True)
                ins.then_inc(sums_ready, 1)

            def project_output(p):
                pe.wait_ge(o_norm_ready, p)
                pe.wait_ge(o_loaded, p * 16)
                for h in range(NQ):
                    ins = pe.matmul(misc_b[:, h * D:(h + 1) * D], o_norm[:, h * P:(h + 1) * P], o_raw[:, :],
                                    start=True, stop=True)
                ins.then_inc(wo_ready, 1)

            def attend(p, t, first=False):
                scores(p, t, first)
                if not first and t == 2:
                    pe.wait_ge(q_stacked, p * 6 + 6)
                    sums(p)
                if not first and t == 5:
                    project_output(p)

            for t in range(HEAD, TILES):
                prepare(0, t)
            values(0, GROUPS - 2)
            values(0, GROUPS - 1)
            for t in range(HEAD):
                attend(0, t, True)
                if t >= 2:
                    weigh(0, t - 2, True)
            with pe.Fori(0, PAIRS - 1) as i:
                for t in range(HEAD, TILES):
                    scores(i, t)
                    prepare(i + 1, t, lambda: weigh(i, t - 2))
                values(i + 1, GROUPS - 2)
                weigh(i, TILES - 2)
                values(i + 1, GROUPS - 1)
                for t in range(HEAD):
                    attend(i + 1, t)
                    if t == 1:
                        weigh(i, TILES - 1)
                    if t >= 2:
                        weigh(i + 1, t - 2)
            for t in range(HEAD, TILES):
                scores(PAIRS - 1, t)
                weigh(PAIRS - 1, t - 2)
            weigh(PAIRS - 1, TILES - 2)
            weigh(PAIRS - 1, TILES - 1)
            pe.wait_ge(x_added, PAIRS)
            sums(PAIRS, last=True)
            project_output(PAIRS)

            transposes(kv_b[0], xn, xn_ready, 4, xt_psum)
            pe.wait_ge(xt_ready, 2)
            pe.wait_ge(w_tail_loaded, 16 * 8)
            pe.wait_ge(consts, ALL_CONSTS)
            for c in range(DC):
                ins = pe.matmul(max_b[0][:, 0:N], w_sk_sb[:, c, :], xt[:, c, :], start=(c == 0), stop=(c == DC - 1))
            ins.then_inc(sproj_ready, 1)
            for f in range(DC):
                for c in range(DC):
                    ins = pe.matmul(kv_b[1][:, f * N:(f + 1) * N], w_sq_sb[:, c, f * P:(f + 1) * P], xt[:, c, :],
                                    start=(c == 0), stop=(c == DC - 1))
            ins.then_inc(sproj_ready, 1)
            for h in range(NQ):
                for c in range(DC):
                    ins = pe.matmul(max_b[1][:, h * SHD:(h + 1) * SHD], xt[:, c, h * P:(h + 1) * P], w_sv_sb[:, c, :],
                                    start=(c == 0), stop=(c == DC - 1))
            ins.then_inc(sproj_ready, 1)
            pe.wait_ge(sq_taken, 1)
            pe.wait_ge(sproj_taken, 3)

            def self_scores(f):
                c, tile = f // 6, 0 if f % 6 < 2 else 1
                heads, nk = fill_shape(f)
                h0 = heads * (f % 6 - (0 if tile == 0 else 2))
                if f >= 3:
                    pe.wait_ge(s_exp, f - 2)
                pe.matmul(bank[f % 3][:, :], sq[:, c, tile * P:(tile + 1) * P], sk_blocks[:, h0:h0 + heads, 0:nk],
                          start=True, stop=False)
                diagonal = bank[f % 3][:, :].rearrange("p (h k) -> p h k", h=heads)[:, :, nk - P:nk]
                pe.matmul(diagonal, ident_b[:, :], diag4[:, 0:heads, :], start=False, stop=True).then_inc(s_scores, 1)

            def self_transposes(f):
                pe.wait_ge(s_exp, f + 1)
                if f >= 2:
                    pe.wait_ge(s_pt_taken, f - 1)
                for b in range(4):
                    ins = pe.transpose(bank[3 + f % 2][:, b * P:(b + 1) * P], sp[:, f, b * P:(b + 1) * P], ident[:, :])
                ins.then_inc(s_pt, 1)

            def self_weigh(f):
                c, tile = f // 6, 0 if f % 6 < 2 else 1
                heads, nk = fill_shape(f)
                h0 = SH8 * c + heads * (f % 6 - (0 if tile == 0 else 2))
                pe.wait_ge(s_pt_taken, f + 1)
                for h in range(heads):
                    o = bank[6 + tile][:, (h0 + h) * (SHD + 1):(h0 + h + 1) * (SHD + 1)]
                    for k in range(nk // P):
                        b = h * (nk // P) + k
                        ins = pe.matmul(o, spt_of(f)[:, b * P:(b + 1) * P], sv[:, k, :], start=(k == 0), stop=(k == nk // P - 1))
                ins.then_inc(s_pv, 1)

            for f in range(12 + 3):
                if f < 12:
                    self_scores(f)
                if 1 <= f < 13:
                    self_transposes(f - 1)
                if f >= 3:
                    self_weigh(f - 3)
            transposes(bank[0], sy, sy_ready, 2, yt_psum)
            pe.wait_ge(yt_ready, 1)
            for h in range(NQ):
                for c in range(DC):
                    ins = pe.matmul(bank[1][:, h * D:(h + 1) * D], yt[:, c, h * P:(h + 1) * P], w_proj_sb[:, c, :],
                                    start=(c == 0), stop=(c == DC - 1))
            ins.then_inc(sproj_out, 1)

            transposes(bank[2], xn, xn_ready, 6, xt_psum)
            pe.wait_ge(xt_ready, 3)
            pe.wait_ge(w2_loaded, 16)
            for e in range(EA + 1):
                if e < EA:
                    if e >= 3:
                        pe.wait_ge(gated_ready, e - 2)
                    for k, w in enumerate((w1_sb, w3_sb)):
                        for c in range(DC):
                            ins = pe.matmul(bank[e % 3][:, k * N:(k + 1) * N], w[:, e, c, :], xt[:, c, :],
                                            start=(c == 0), stop=(c == DC - 1))
                    ins.then_inc(h_ready, 1)
                if e == 0:
                    for h in range(NQ):
                        for c in range(DC):
                            ins = pe.matmul(bank[3][:, h * E:(h + 1) * E], xt[:, c, h * P:(h + 1) * P],
                                            router_w_sb[:, c, :], start=(c == 0), stop=(c == DC - 1))
                    ins.then_inc(router_ready, 1)
                if e >= 1:
                    d = e - 1
                    pe.wait_ge(gated_ready, d + 1)
                    if d == 0:
                        pe.wait_ge(gap_ready, 1)
                    for h in range(NQ):
                        if d >= 2 and h == 0:
                            pe.wait_ge(expert_added, d - 1)
                        ins = pe.matmul(bank[3 + d % 2][:, h * D:(h + 1) * D], gated[:, d, h * P:(h + 1) * P], w2_sb[:, d, :],
                                        start=True, stop=True)
                    ins.then_inc(expert_out, 1)


def kernel(**inputs):
    import concourse.bacc as _bacc
    from concourse import mybir as _mybir
    from concourse.bass_utils import run_bass_kernel_spmd as _run

    a = {k: np.asarray(v) for k, v in inputs.items()}

    def by_pair(w):
        w = w.reshape(w.shape[0], PAIRS, P).transpose(1, 0, 2)
        return np.concatenate([w, w[-1:]], axis=0)

    wk, wv = by_pair(a["L0_xattn_Wk"]), by_pair(a["L0_xattn_Wv"])
    w_attn = a["L0_attn_w_attn"]
    arrays = {
        "x": a["x"][0],
        "ctx_main": a["ctx_768"][0].T[0:P],
        "ctx_tail": a["ctx_768"][0].T[P:CD],
        "w_kv": np.concatenate([part for w in (wk, wv) for part in (w[:, 0:P], np.concatenate([w[:, P:CD]] * 2, axis=1))], axis=2),
        "w_q": by_pair(a["L0_xattn_Wq"]).reshape(PAIRS + 1, DC, P, P).transpose(0, 2, 1, 3),
        "w_o": a["L0_xattn_Wo"].reshape(PAIRS, P, D),
        "bo": a["L0_xattn_bo"],
        "w_sq": w_attn[:, 0:D],
        "w_sk": np.concatenate([w_attn[:, D:D + SHD]] * SH8, axis=1),
        "w_sv": w_attn[:, D + SHD:D + 2 * SHD],
        "w_proj": a["L0_attn_w_proj"],
        "router_w": a["L0_ffn_router_w"],
        "router_b": a["L0_ffn_router_b"],
        "w1": np.concatenate([a["L0_ffn_routed_w1"], a["L0_ffn_shared_w1"]], axis=0),
        "w3": np.concatenate([a["L0_ffn_routed_w3"], a["L0_ffn_shared_w3"]], axis=0),
        "w2": np.concatenate([a["L0_ffn_routed_w2"], a["L0_ffn_shared_w2"]], axis=0),
    }
    arrays = {f"in_{k}": np.ascontiguousarray(v) for k, v in arrays.items()}
    nc = _bacc.Bacc("TRN2", target_bir_lowering=False, num_devices=1)
    args = [nc.dram_tensor(k, v.shape, _mybir.dt.from_np(v.dtype), kind="ExternalInput").ap() for k, v in arrays.items()]
    out = nc.dram_tensor("out", (N, D), F32, kind="ExternalOutput").ap()
    build(nc, *args, out)
    r = _run(nc, [arrays], core_ids=[0])
    return r.results[0]["out"].reshape(1, N, D)
```

```python
from contextlib import ExitStack

import concourse.bass as bass
import numpy as np
from concourse import mybir

F32 = mybir.dt.float32
F16 = mybir.dt.float16
BF16 = mybir.dt.bfloat16
U32 = mybir.dt.uint32
ALU = mybir.AluOpType
ACT = mybir.ActivationFunctionType
AX_X = mybir.AxisListType.X

P = 128
N = 256
NQ = N // P
D = 256
DC = D // P
M = 4096
CD = 192
HEADS = 16
HD = 64
PAIRS = HEADS // 2
TILES = M // P
CHUNK = 512
CHUNKS = M // CHUNK
GROUP = 4
GROUPS = TILES // GROUP
RESTACK = 1024
RESTACKS = M // RESTACK
PROBS = 8
W_SCALE = 256.0
MAX_UNIT = 64.0
Q_SCALE = float(HD) ** -0.5
EPS = 1e-5

SHD = 16
SH8 = P // SHD
S_SCALE = float(SHD) ** -0.5
MASKED = -1e30
E = 8
ES = 2
EA = E + ES
H = 128

HEAD = 8
Q_STEP = 8
K_STEP = 9
MAX_STEP = 11
V_STEP = 17
M4_STEP = 27
ROWS_STEP = 29
MAXES = 2 * NQ * CHUNKS
IDENT_CONSTS, ZERO_CONSTS, QK_CONSTS, ALL_CONSTS = 6, 8, 11, 17
MAX_UNITS = float(np.array([MAX_UNIT] * 2, np.float16).view(np.float32)[0])
HI_LAG, LO_LAG = 2, 4
O_COLS = 2 * HD + 1
V_COLS = O_COLS + 1
P_SCALE = 64.0
A1, B1, A2, B2 = range(4)


def build(nc, x, ctx_main, ctx_tail, w_kv, w_q, w_o, bo, w_sq, w_sk, w_sv, w_proj, router_w,
          router_b, w1, w3, w2, out):
    with ExitStack() as stack:
        def sb(name, shape, dt):
            return stack.enter_context(nc.sbuf_tensor(name, shape, dt))

        def sem(name):
            return stack.enter_context(nc.semaphore(name))

        ctx_hi = sb("ctx_hi", [P, M], F16)
        ctx_lo = sb("ctx_lo", [P, M], F16)
        ctx_st = sb("ctx_st", [P, M], F16)
        k_hi = sb("k_hi", [P, M], F16)
        k_lo = sb("k_lo", [P, M], F16)
        k_st = sb("k_st", [P, 4, M], F16)
        v = sb("v", [P, TILES, 2, V_COLS], F16)
        v_f32 = v[:, :, :, :].rearrange("p t a n -> p (t a n)").bitcast(F32)
        probs = sb("probs", [P, PROBS, 2 * N], F32)
        probs_hi = sb("probs_hi", [P, PROBS, 2 * N], F16)
        probs_lo = sb("probs_lo", [P, PROBS, 2 * N], F16)
        kv_raw = sb("kv_raw", [P, 4 * P], F32)
        kv_hi = sb("kv_hi", [P, 4 * P], F16)
        kv_lo = sb("kv_lo", [P, 4 * P], F16)
        q_raw = sb("q_raw", [P, DC, P], F32)
        o_raw = sb("o_raw", [P, D], F32)
        q_nat = sb("q_nat", [P, 2, N], F16)
        q_st = sb("q_st", [P, 4, N], F16)
        max_part = sb("max_part", [P, 2 * NQ, CHUNKS], F32)
        max4 = sb("max4", [P, 2 * NQ], F32)
        neg_max = sb("neg_max", [P, 2 * NQ], F16)
        o_parts = sb("o_parts", [P, 2, NQ, O_COLS], F32)
        inv_sum = sb("inv_sum", [P, 2, NQ, 1], F32)
        o_both = sb("o_both", [P, 2, NQ, HD], F32)
        o_norm = sb("o_norm", [P, NQ, 2, HD], F32)
        o_norm_t = sb("o_norm_t", [P, N], F32)
        ident = sb("ident", [P, P], F32)
        ident_h = sb("ident_h", [P, P], F16)
        ident_b = sb("ident_b", [P, P], BF16)
        xs = sb("xs", [P, NQ, D], F32)
        x_in = sb("x_in", [P, NQ, D], F32)
        bo_all = sb("bo_all", [P, D], F32)
        xn = sb("xn", [P, NQ, D], F32)
        xt = sb("xt", [P, DC, N], F32)
        stats = sb("stats", [P, NQ, 6], F32)
        mean_var = sb("mean_var", [P, NQ, 2], F32)
        std = sb("std", [P, NQ], F32)
        inv_std = sb("inv_std", [P, NQ], F32)
        w_sq_sb = sb("w_sq_sb", [P, DC, D], F32)
        w_sk_sb = sb("w_sk_sb", [P, DC, P], F32)
        w_sv_sb = sb("w_sv_sb", [P, DC, SHD], F32)
        w_proj_sb = sb("w_proj_sb", [P, DC, D], F32)
        head_rows = sb("head_rows", [P, SH8], F32)
        diag4 = sb("diag4", [P, 4, P], BF16)
        sq = sb("sq", [P, DC, N], F32)
        sv = sb("sv", [P, NQ, SHD + 1], F32)
        smax = sb("smax", [P, 12, 4], F32)
        sneg = sb("sneg", [P, 12, 4], F32)
        sinv = sb("sinv", [P, NQ, HEADS], F32)
        sy = sb("sy", [P, NQ, D], F32)
        k_st_f32 = k_st[:, :, :].rearrange("p a m -> p (a m)").bitcast(F32)
        sp = k_st_f32[:, 0:12 * 512].rearrange("p (f n) -> p f n", n=512)
        sk_blocks = k_st_f32[:, 12 * 512:16 * 512].rearrange("p (h n) -> p h n", h=SH8)
        spt = v_f32[:, 0:8 * 512].rearrange("p (f n) -> p f n", n=512)
        yt = sb("yt", [P, DC, N], F32)
        router_w_sb = sb("router_w_sb", [P, DC, E], F32)
        router_b_sb = sb("router_b_sb", [P, E], F32)
        expert_no = sb("expert_no", [P, E], F32)
        logits = sb("logits", [P, NQ, E], F32)
        top8 = sb("top8", [P, NQ, 8], F32)
        top_at = sb("top_at", [P, NQ, 8], U32)
        top_no = sb("top_no", [P, NQ, 2], F32)
        gap = sb("gap", [P, NQ], F32)
        e_gap = sb("e_gap", [P, NQ], F32)
        e_gap1 = sb("e_gap1", [P, NQ], F32)
        gate12 = sb("gate12", [P, NQ, 2], F32)
        first_gate = sb("first_gate", [P, NQ, E], F32)
        second_gate = sb("second_gate", [P, NQ, E], F32)
        gates = sb("gates", [P, NQ, E], F32)
        w1_sb = sb("w1_sb", [P, EA, DC, H], F32)
        w3_sb = sb("w3_sb", [P, EA, DC, H], F32)
        w2_sb = sb("w2_sb", [P, EA, D], F32)
        act_h = sb("act_h", [P, 2, N], F32)

        bank = [stack.enter_context(nc.psum_tensor(f"bank{i}", [P, 512], F32)) for i in range(8)]
        score_b = bank[0:2]
        out_b = (bank[2], bank[7])
        kv_b = bank[3:5]
        max_b = bank[5:7]

        x_loaded, bo_loaded, w_tail_loaded = sem("x_loaded"), sem("bo_loaded"), sem("w_tail_loaded")
        w2_loaded = sem("w2_loaded")
        ctx_loaded = [sem(f"ctx_loaded{i}") for i in range(RESTACKS)]
        kv_loaded, q_loaded, o_loaded = sem("kv_loaded"), sem("q_loaded"), sem("o_loaded")
        restacked = [sem(f"restacked{i}") for i in range(RESTACKS)]
        ctx_hi_ready, ctx_lo_ready, ctx_pool_lo = sem("ctx_hi_ready"), sem("ctx_lo_ready"), sem("ctx_pool_lo")
        consts = sem("consts")
        w_split = sem("w_split")
        q_ready, q_taken = sem("q_ready"), sem("q_taken")
        kv_ready = sem("kv_ready")
        k_hi_ready, k_lo_ready = sem("k_hi_ready"), sem("k_lo_ready")
        v_hi_ready, v_lo_ready = sem("v_hi_ready"), sem("v_lo_ready")
        max_ready, max_taken = sem("max_ready"), sem("max_taken")
        max4_ready, neg_max_ready = sem("max4_ready"), sem("neg_max_ready")
        rows_ready = sem("rows_ready")
        q_stacked = sem("q_stacked")
        scores_ready, probs_ready = sem("scores_ready"), sem("probs_ready")
        hi_ready, lo_ready = sem("hi_ready"), sem("lo_ready")
        lo_odd_ready = sem("lo_odd_ready")
        hi_weighed, lo_weighed = sem("hi_weighed"), sem("lo_weighed")
        out_taken, o_chain = sem("out_taken"), sem("o_chain")
        o_transposed, o_norm_t_ready = sem("o_transposed"), sem("o_norm_t_ready")
        o_norm_ready, wo_ready, x_added = sem("o_norm_ready"), sem("wo_ready"), sem("x_added")
        var_ready, std_ready, xn_ready = sem("var_ready"), sem("std_ready"), sem("xn_ready")
        xt_psum, xt_ready = sem("xt_psum"), sem("xt_ready")
        sproj_ready, sproj_taken, sq_taken = sem("sproj_ready"), sem("sproj_taken"), sem("sq_taken")
        s_scores, s_neg, s_exp = sem("s_scores"), sem("s_neg"), sem("s_exp")
        s_pt, s_pt_taken, s_pv = sem("s_pt"), sem("s_pt_taken"), sem("s_pv")
        sy_ready, yt_psum, yt_ready, sproj_out = sem("sy_ready"), sem("yt_psum"), sem("yt_ready"), sem("sproj_out")
        router_ready, gap_ready, gap_exp = sem("router_ready"), sem("gap_ready"), sem("gap_exp")
        h_ready, silu_ready, gated_ready = sem("h_ready"), sem("silu_ready"), sem("gated_ready")
        expert_out, expert_added = sem("expert_out"), sem("expert_added")
        dve_step = sem("dve_step")
        stored = sem("stored")

        block = stack.enter_context(nc.Block())

        def v_part(g, at):
            return v[:, GROUP * g:GROUP * (g + 1), :, at:at + HD].rearrange("p t a n -> p (t a) n")

        def kv_group(g):
            return kv_b[g % 2][:, :].rearrange("p (t n) -> p t n", n=HD)

        def raw_chunk(j):
            if j < 2:
                flat = probs[:, :, :].rearrange("p b n -> p (b n)")
            else:
                flat = v_f32
            at = (j % 2) * 2 * RESTACK
            return flat[:, at:at + RESTACK], flat[:, at + RESTACK:at + 2 * RESTACK]

        def wait_ctx_split(engine, j):
            engine.wait_ge(ctx_hi_ready, 2 * (j + 1))
            engine.wait_ge(ctx_lo_ready, min(j + 1, 2))
            engine.wait_ge(ctx_pool_lo, j + 1 if j < 2 else 2 * j)

        def wait_lo(engine, p, t, last):
            if not last or t < HEAD:
                engine.wait_ge(lo_ready, p * TILES + t + 1)
            elif t % 2 == 0:
                engine.wait_ge(lo_ready, p * TILES + HEAD + (t - HEAD) // 2 + 1)
            else:
                engine.wait_ge(lo_odd_ready, (t - HEAD) // 2 + 1)

        def tokens(first, count):
            return slice(first, first + count)

        def fill_shape(f):
            return (4, P) if f % 6 < 2 else (2, 2 * P)

        def gated(e):
            part = (ctx_hi, ctx_lo)[e // 8][:, :].bitcast(F32)
            return part[:, (e % 8) * N:(e % 8 + 1) * N]

        def spt_of(f):
            if f < 8:
                return spt[:, f, :]
            part = (k_hi, k_lo)[(f - 8) // 2][:, :].bitcast(F32)
            return part[:, ((f - 8) % 2) * 512:((f - 8) % 2 + 1) * 512]

        def repeated(ap, n):
            return ap.rearrange("p (a m) -> p a m", a=1).broadcast_to([ap.shape[0], n, ap.shape[1]])

        @block.sync
        def _(sp_q):
            sp_q.dma_start(x_in[:, :, :], x.rearrange("(h p) d -> p h d", p=P)).then_inc(x_loaded, 16)
            sp_q.dma_start(kv_raw[:, :], w_kv[0]).then_inc(kv_loaded, 16)
            sp_q.dma_start(q_raw[:, :, :], w_q[0]).then_inc(q_loaded, 16)

            def load_ctx(j):
                sl = tokens(RESTACK * j, RESTACK)
                main, tail = raw_chunk(j)
                sp_q.dma_start(main, ctx_main[:, sl]).then_inc(ctx_loaded[j], 16)
                sp_q.dma_start(tail[0:HD, :], ctx_tail[:, sl]).then_inc(ctx_loaded[j], 16)
                sp_q.dma_start(tail[HD:P, :], ctx_tail[:, sl]).then_inc(ctx_loaded[j], 16)

            load_ctx(0)
            load_ctx(1)
            sp_q.dma_start(bo_all[:, :], bo.rearrange("(a d) -> a d", a=1).broadcast_to([P, D])).then_inc(bo_loaded, 16)
            load_ctx(2)
            load_ctx(3)
            sp_q.wait_ge(w_split, 2)
            sp_q.dma_start(kv_raw[:, :], w_kv[1]).then_inc(kv_loaded, 16)
            sp_q.wait_ge(q_ready, 1)
            sp_q.dma_start(q_raw[:, :, :], w_q[1]).then_inc(q_loaded, 16)

            def restack(g, parts, former_scores=None):
                sp_q.wait_ge(k_lo_ready, parts)
                sp_q.wait_ge(k_hi_ready, parts)
                if former_scores is not None:
                    sp_q.wait_ge(scores_ready, former_scores)
                sl = tokens(RESTACK * g, RESTACK)
                for rows, to, which, part in (
                    (slice(0, HD), slice(0, HD), A1, k_hi), (slice(0, HD), slice(0, HD), A2, k_hi),
                    (slice(HD, P), slice(HD, P), B1, k_hi), (slice(HD, P), slice(HD, P), B2, k_hi),
                    (slice(0, HD), slice(HD, P), A1, k_lo), (slice(HD, P), slice(0, HD), B1, k_lo),
                ):
                    sp_q.dma_start(k_st[to, which, sl], part[rows, sl]).then_inc(restacked[g], 16)

            sp_q.wait_ge(consts, ZERO_CONSTS)
            for g in range(RESTACKS):
                restack(g, 2 * (g + 1))
            for to, frm in (
                (w_sq_sb[:, :, :], w_sq.rearrange("(c p) n -> p c n", p=P)),
                (w_sk_sb[:, :, :], w_sk.rearrange("(c p) n -> p c n", p=P)),
                (w_sv_sb[:, :, :], w_sv.rearrange("(c p) n -> p c n", p=P)),
                (w_proj_sb[:, :, :], w_proj.rearrange("(c p) n -> p c n", p=P)),
                (router_w_sb[:, :, :], router_w.rearrange("(c p) n -> p c n", p=P)),
                (router_b_sb[:, :], router_b.rearrange("(a d) -> a d", a=1).broadcast_to([P, E])),
                (w1_sb[:, :, :, :], w1.rearrange("e (c p) h -> p e c h", p=P)),
                (w3_sb[:, :, :, :], w3.rearrange("e (c p) h -> p e c h", p=P)),
            ):
                sp_q.dma_start(to, frm).then_inc(w_tail_loaded, 16)
            sp_q.dma_start(w2_sb[:, :, :], w2.rearrange("e h d -> h e d")).then_inc(w2_loaded, 16)

            with sp_q.Fori(0, PAIRS - 1) as i:
                def now(value):
                    return sp_q.snap(sp_q.to_reg(value))

                after_next = now(i + 2)
                split = now(i * 2 + 4)
                parts = [now((i + 1) * CHUNKS + 2 * (g + 1)) for g in range(RESTACKS)]
                former = [now(i * TILES + 8 * (g + 1)) for g in range(RESTACKS)]
                w_o_i = w_o[bass.ds(i, 1), :, :].rearrange("a p d -> (a p) d")
                w_kv_i = w_kv[bass.ds(after_next, 1), :, :].rearrange("a p d -> (a p) d")
                w_q_i = w_q[bass.ds(after_next, 1), :, :, :].rearrange("a p c d -> (a p) c d")
                sp_q.wait_ge(x_added, i + 1)
                sp_q.dma_start(o_raw[:, :], w_o_i).then_inc(o_loaded, 16)
                sp_q.wait_ge(w_split, split)
                sp_q.dma_start(kv_raw[:, :], w_kv_i).then_inc(kv_loaded, 16)
                sp_q.wait_ge(q_ready, after_next)
                sp_q.dma_start(q_raw[:, :, :], w_q_i).then_inc(q_loaded, 16)
                for g in range(RESTACKS):
                    restack(g, parts[g], former[g])
            sp_q.wait_ge(wo_ready, PAIRS - 1)
            sp_q.dma_start(o_raw[:, :], w_o[PAIRS - 1]).then_inc(o_loaded, 16)
            sp_q.wait_ge(kv_loaded, 16 * (PAIRS + 1))
            sp_q.wait_ge(q_loaded, 16 * (PAIRS + 1))

            sp_q.wait_ge(expert_added, EA)
            sp_q.dma_start(out.rearrange("(h p) d -> p h d", p=P), xs[:, :, :]).then_inc(stored, 16)
            sp_q.wait_ge(stored, 16)

        @block.gpsimd
        def _(pool):
            made = [0]

            def const(ins):
                made[0] += 1
                ins.then_inc(consts, 1)
                pool.wait_ge(consts, made[0])

            for m in (ident, ident_h, ident_b):
                const(pool.memset(m[:, :], 0.0))
                const(pool.affine_select(out=m[:, :], in_=m[:, :], compare_op=ALU.not_equal, fill=1.0, base=0,
                                         pattern=[[-1, P]], channel_multiplier=1))
            const(pool.memset(k_st[:, A2:B2 + 1, :].rearrange("p a m -> p (a m)").bitcast(F32), 0.0))
            const(pool.memset(q_st[:, A2:B2 + 1, :], 0.0))
            split = 0
            for j in range(RESTACKS):
                sl = tokens(RESTACK * j, RESTACK)
                main, tail = raw_chunk(j)
                pool.wait_ge(ctx_loaded[j], 48)
                if j >= 2:
                    pool.wait_ge(ctx_hi_ready, 2 * j + 1)
                    pool.tensor_tensor(ctx_lo[:, sl], main, ctx_hi[:, sl], ALU.subtract).then_inc(ctx_pool_lo, 1)
                    split += 1
                    pool.wait_ge(ctx_pool_lo, split)
                pool.wait_ge(ctx_hi_ready, 2 * j + 2)
                pool.tensor_tensor(ctx_st[HD:P, sl], tail[HD:P, :], ctx_st[HD:P, sl],
                                   ALU.subtract).then_inc(ctx_pool_lo, 1)
                split += 1
                pool.wait_ge(ctx_pool_lo, split)
            const(pool.memset(k_st[HD:HD + 1, A2, :].bitcast(F32), MAX_UNITS))
            const(pool.memset(k_st[0:1, B2, :].bitcast(F32), MAX_UNITS))
            const(pool.memset(v[:, :, :, 2 * HD:2 * HD + 1], 1.0))
            const(pool.memset(diag4[:, :, :], 0.0))
            const(pool.affine_select(out=diag4[:, :, :], in_=diag4[:, :, :], compare_op=ALU.is_ge,
                                     fill=MASKED, base=0, pattern=[[0, 4], [-1, P]], channel_multiplier=1))
            const(pool.memset(head_rows[:, :], 1.0))
            const(pool.affine_select(out=head_rows[:, :], in_=head_rows[:, :], compare_op=ALU.is_ge,
                                     fill=0.0, base=0, pattern=[[-SHD, SH8]], channel_multiplier=1))
            const(pool.affine_select(out=head_rows[:, :], in_=head_rows[:, :], compare_op=ALU.is_ge,
                                     fill=0.0, base=SHD - 1, pattern=[[SHD, SH8]], channel_multiplier=-1))
            const(pool.iota(expert_no[:, :], pattern=[[1, E]], base=0, channel_multiplier=0,
                            allow_small_or_imprecise_dtypes=True))

            def step(p, t, first=False):
                pool.wait_ge(hi_ready, p * TILES + t + 1)
                if not first:
                    pool.wait_ge(lo_weighed, p * TILES + t + 1 - PROBS)
                pool.tensor_tensor(probs_lo[:, t % PROBS, :], probs[:, t % PROBS, :], probs_hi[:, t % PROBS, :],
                                   ALU.subtract).then_inc(lo_ready, 1)

            for t in range(HEAD):
                step(0, t, True)
            with pool.Fori(0, PAIRS - 1) as i:
                for t in range(HEAD, TILES):
                    step(i, t)
                for t in range(HEAD):
                    step(i + 1, t)
            for t in range(HEAD, TILES, 2):
                step(PAIRS - 1, t)

        @block.scalar
        def _(act):
            def sqrt_var(k):
                act.wait_ge(var_ready, k)
                act.activation(std[:, :], mean_var[:, :, 1], ACT.Sqrt).then_inc(std_ready, 1)

            sqrt_var(1)

            def split_ctx(j):
                act.wait_ge(ctx_loaded[j], 48)
                sl = tokens(RESTACK * j, RESTACK)
                main, tail = raw_chunk(j)
                act.copy(ctx_hi[:, sl], main).then_inc(ctx_hi_ready, 1)
                act.copy(ctx_st[:, sl], tail).then_inc(ctx_hi_ready, 1)

            def step(p, t, first=False, last=False):
                act.wait_ge(scores_ready, p * TILES + t + 1)
                if not first:
                    wait_lo(act, p, t - PROBS, last)
                act.activation(probs[:, t % PROBS, :], score_b[t % 2][:, :], ACT.Exp).then_inc(probs_ready, 1)
                if last:
                    return
                if not first:
                    act.wait_ge(hi_weighed, p * TILES + t + 1 - PROBS)
                act.activation(probs_hi[:, t % PROBS, :], score_b[t % 2][:, :], ACT.Exp).then_inc(hi_ready, 1)

            def prepare(n, t, former=True):
                if K_STEP <= t < K_STEP + CHUNKS:
                    c = t - K_STEP
                    act.wait_ge(kv_ready, n * (CHUNKS + GROUPS) + c + 1)
                    if former:
                        act.wait_ge(restacked[c // 2], n * 96)
                        act.wait_ge(max_ready, n * MAXES)
                    act.activation(k_hi[:, tokens(CHUNK * c, CHUNK)], kv_b[c % 2][:, :], ACT.Copy,
                                   scale=1.0 / W_SCALE).then_inc(k_hi_ready, 1)
                if V_STEP <= t < V_STEP + 2 * (GROUPS - 2) and (t - V_STEP) % 2 == 0:
                    values(n, (t - V_STEP) // 2, former)

            def values(n, g, former=True):
                act.wait_ge(kv_ready, n * (CHUNKS + GROUPS) + CHUNKS + g + 1)
                if former:
                    act.wait_ge(lo_weighed, (n - 1) * TILES + GROUP * (g + 1))
                elif g == 0:
                    wait_ctx_split(act, RESTACKS - 1)
                act.activation(v_part(g, HD), kv_group(g), ACT.Copy, scale=1.0 / W_SCALE).then_inc(v_hi_ready, 1)

            split_ctx(0)
            split_ctx(1)
            for t in range(HEAD, TILES):
                prepare(0, t, False)
                if t in (K_STEP, K_STEP + 2):
                    split_ctx((t - K_STEP) // 2 + 2)
            values(0, GROUPS - 2, False)
            values(0, GROUPS - 1, False)
            for t in range(HEAD):
                step(0, t, True)
            with act.Fori(0, PAIRS - 1) as i:
                for t in range(HEAD, TILES):
                    step(i, t)
                    prepare(i + 1, t)
                values(i + 1, GROUPS - 2)
                for t in range(HEAD):
                    step(i + 1, t)
                    if t == 1:
                        values(i + 1, GROUPS - 1)
            for t in range(HEAD, TILES):
                step(PAIRS - 1, t, last=True)

            sqrt_var(2)
            act.wait_ge(sproj_ready, 2)
            act.activation(sq[:, :, :].rearrange("p c n -> p (c n)"), kv_b[1][:, :], ACT.Copy,
                           scale=S_SCALE).then_inc(sq_taken, 1)
            for f in range(12):
                heads, keys = fill_shape(f)
                act.wait_ge(s_neg, f + 1)
                for h in range(heads):
                    last = act.activation(sp[:, f, h * keys:(h + 1) * keys],
                                          bank[f % 3][:, h * keys:(h + 1) * keys], ACT.Exp,
                                          bias=sneg[:, f, h:h + 1])
                last.then_inc(s_exp, 1)
            sqrt_var(3)
            act.wait_ge(gap_ready, 1)
            act.activation(e_gap[:, :], gap[:, :], ACT.Exp).then_inc(gap_exp, 1)
            for e in range(EA):
                act.wait_ge(h_ready, e + 1)
                if e >= 2:
                    act.wait_ge(gated_ready, e - 1)
                act.activation(act_h[:, e % 2, :], bank[e % 3][:, 0:N], ACT.Silu).then_inc(silu_ready, 1)

        @block.vector
        def _(dve):
            chain = [0]

            def link(ins):
                chain[0] += 1
                ins.then_inc(dve_step, 1)
                dve.wait_ge(dve_step, chain[0])

            def layernorm(src, k):
                for h in range(NQ):
                    link(dve.bn_stats(stats[:, h, :], src[:, h, :]))
                    link(dve.bn_aggr(mean_var[:, h, :], stats[:, h, :]))
                dve.tensor_scalar(mean_var[:, :, 1], mean_var[:, :, 1], EPS, None, ALU.add).then_inc(var_ready, 1)
                dve.wait_ge(std_ready, k)
                link(dve.reciprocal(inv_std[:, :], std[:, :]))
                for h in range(NQ):
                    dve.tensor_scalar(xn[:, h, :], src[:, h, :], mean_var[:, h, 0:1], inv_std[:, h:h + 1],
                                      ALU.subtract, ALU.mult).then_inc(xn_ready, 1)

            def transposed(src_bank, k):
                dve.wait_ge(xt_psum, k)
                dve.tensor_copy(xt[:, :, :].rearrange("p c n -> p (c n)"), src_bank[:, :]).then_inc(xt_ready, 1)

            dve.wait_ge(x_loaded, 16)
            layernorm(x_in, 1)
            transposed(out_b[0], 1)

            def split_ctx(j):
                sl = tokens(RESTACK * j, RESTACK)
                dve.wait_ge(ctx_loaded[j], 48)
                dve.wait_ge(ctx_hi_ready, 2 * j + 1)
                dve.tensor_tensor(ctx_lo[:, sl], raw_chunk(j)[0], ctx_hi[:, sl], ALU.subtract).then_inc(ctx_lo_ready, 1)

            def split_weights(n, former=True):
                dve.wait_ge(kv_loaded, n * 16 + 16)
                if former:
                    dve.wait_ge(kv_ready, n * (CHUNKS + GROUPS))
                dve.tensor_scalar(kv_hi[:, :], kv_raw[:, :], W_SCALE, None, ALU.mult).then_inc(w_split, 1)
                dve.wait_ge(w_split, n * 2 + 1)
                dve.scalar_tensor_tensor(kv_lo[:, :], kv_raw[:, :], W_SCALE, kv_hi[:, :],
                                         ALU.mult, ALU.subtract).then_inc(w_split, 1)

            def split_queries(n, former=True):
                dve.wait_ge(q_ready, n + 1)
                if former:
                    dve.wait_ge(max_ready, n * MAXES)
                    dve.wait_ge(q_stacked, n * 6)
                dve.tensor_scalar(q_nat[:, 0, :], kv_b[1][:, 0:N], Q_SCALE, None, ALU.mult).then_inc(q_taken, 1)
                dve.wait_ge(q_taken, n * 2 + 1)
                dve.scalar_tensor_tensor(q_nat[:, 1, :], kv_b[1][:, 0:N], Q_SCALE, q_nat[:, 0, :],
                                         ALU.mult, ALU.subtract).then_inc(q_taken, 1)

            def prepare(n, t, former=True):
                if t == Q_STEP:
                    split_weights(n, former)
                    split_queries(n, former)
                def part_max(j):
                    dve.wait_ge(max_ready, n * MAXES + j + 1)
                    if former and j == 0:
                        dve.wait_ge(max4_ready, n)
                    dve.tensor_reduce(max_part[:, j % 4, j // 4:j // 4 + 1], max_b[j % 2][:, :], AX_X,
                                      ALU.max).then_inc(max_taken, 1)

                maxes = MAX_STEP <= t < MAX_STEP + MAXES // 2
                if maxes:
                    part_max(2 * (t - MAX_STEP))
                if K_STEP <= t < K_STEP + CHUNKS:
                    c = t - K_STEP
                    sl = tokens(CHUNK * c, CHUNK)
                    dve.wait_ge(k_hi_ready, n * CHUNKS + c + 1)
                    if former:
                        dve.wait_ge(restacked[c // 2], n * 96)
                    dve.scalar_tensor_tensor(k_lo[:, sl], kv_b[c % 2][:, :], 1.0 / W_SCALE, k_hi[:, sl],
                                             ALU.mult, ALU.subtract).then_inc(k_lo_ready, 1)
                if V_STEP < t <= V_STEP + 2 * (GROUPS - 2) and (t - V_STEP) % 2 == 1:
                    values(n, (t - V_STEP) // 2)
                if maxes:
                    part_max(2 * (t - MAX_STEP) + 1)
                if t == M4_STEP:
                    dve.wait_ge(max_taken, n * MAXES + MAXES)
                    if former:
                        dve.wait_ge(neg_max_ready, n)
                        dve.wait_ge(rows_ready, n)
                    dve.tensor_reduce(max4[:, :], max_part[:, :, :], AX_X, ALU.max).then_inc(max4_ready, 1)
                    dve.wait_ge(max4_ready, n + 1)
                    dve.tensor_scalar(neg_max[:, :], max4[:, :], -1.0 / MAX_UNIT, float(np.log(P_SCALE)) / MAX_UNIT,
                                      ALU.mult, ALU.add).then_inc(neg_max_ready, 1)

            def values(n, g):
                dve.wait_ge(v_hi_ready, n * GROUPS + g + 1)
                dve.scalar_tensor_tensor(v_part(g, 0), kv_group(g), 1.0 / W_SCALE, v_part(g, HD),
                                         ALU.mult, ALU.subtract).then_inc(v_lo_ready, 1)

            def stack_queries(n, former=True):
                if former:
                    dve.wait_ge(scores_ready, n * TILES)
                dve.wait_ge(q_taken, n * 2 + 2)
                dve.tensor_copy(q_st[0:HD, A1:B2 + 1:2, :], q_nat[0:HD, :, :]).then_inc(q_stacked, 1)
                dve.tensor_copy(q_st[HD:P, B1:B2 + 1:2, :], q_nat[HD:P, :, :]).then_inc(q_stacked, 1)
                dve.tensor_copy(q_st[HD:P, A1, :], q_nat[0:HD, 0, :]).then_inc(q_stacked, 1)
                dve.tensor_copy(q_st[0:HD, B1, :], q_nat[HD:P, 0, :]).then_inc(q_stacked, 1)
                dve.wait_ge(rows_ready, n + 1)
                dve.tensor_copy(q_st[HD:HD + 1, A2, :], max_b[0][HD:HD + 1, 0:N]).then_inc(q_stacked, 1)
                dve.tensor_copy(q_st[0:1, B2, :], max_b[0][0:1, 0:N]).then_inc(q_stacked, 1)

            def take_output(p):
                dve.wait_ge(lo_weighed, p * TILES + TILES)
                dve.wait_ge(x_added, p + 1)
                for a in range(2):
                    dve.tensor_copy(o_parts[:, a, :, :].rearrange("p h n -> p (h n)"),
                                    out_b[a][:, 0:NQ * O_COLS]).then_inc(out_taken, 1)

            def normalise(p):
                dve.wait_ge(out_taken, 2 * p)
                dve.reciprocal(inv_sum[:, :, :, :], o_parts[:, :, :, 2 * HD:2 * HD + 1]).then_inc(o_chain, 1)
                dve.tensor_tensor(o_both[:, :, :, :], o_parts[:, :, :, HD:2 * HD], o_parts[:, :, :, 0:HD],
                                  ALU.add).then_inc(o_chain, 1)
                dve.wait_ge(o_chain, 2 * p)
                dve.wait_ge(x_added, p)
                for a in range(2):
                    ins = dve.tensor_tensor(o_norm[:, :, a, :], o_both[:, a, :, :],
                                            inv_sum[:, a, :, :].broadcast_to([P, NQ, HD]), ALU.mult)
                ins.then_inc(o_norm_ready, 1)

            def take_transposed(p):
                dve.wait_ge(o_transposed, p)
                dve.tensor_copy(o_norm_t[:, :], kv_b[1][:, 0:N]).then_inc(o_norm_t_ready, 1)

            def add_output(p):
                dve.wait_ge(wo_ready, p)
                dve.wait_ge(x_added, p)
                dve.tensor_tensor(xs[:, :, :].rearrange("p h d -> p (h d)"), kv_b[0][:, :],
                                  xs[:, :, :].rearrange("p h d -> p (h d)"), ALU.add).then_inc(x_added, 1)

            def finish(p, t):
                if t == 2:
                    normalise(p)
                    values(p, GROUPS - 1)
                if t == 4:
                    take_transposed(p)
                if t == 6:
                    add_output(p)

            split_weights(0, False)
            split_ctx(0)
            split_queries(0, False)
            for t in range(K_STEP, TILES):
                if t == K_STEP:
                    split_ctx(1)
                prepare(0, t, False)
            dve.wait_ge(bo_loaded, 16)
            for h in range(NQ):
                ins = dve.tensor_tensor(xs[:, h, :], x_in[:, h, :], bo_all[:, :], ALU.add)
            ins.then_inc(x_added, 1)
            dve.wait_ge(consts, QK_CONSTS)
            values(0, GROUPS - 2)
            stack_queries(0, False)
            values(0, GROUPS - 1)
            with dve.Fori(0, PAIRS - 1) as i:
                for t in range(HEAD, TILES):
                    prepare(i + 1, t)
                stack_queries(i + 1)
                values(i + 1, GROUPS - 2)
                take_output(i)
                for t in range(HEAD):
                    finish(i + 1, t)
            for t in range(HEAD, TILES):
                n = (PAIRS - 1) * TILES + t + 1
                dve.wait_ge(probs_ready, n)
                dve.wait_ge(hi_weighed, n - PROBS)
                wait_lo(dve, PAIRS - 1, t - PROBS, True)
                dve.tensor_copy(probs_hi[:, t % PROBS, :], probs[:, t % PROBS, :]).then_inc(hi_ready, 1)
                if t % 2 == 1:
                    dve.wait_ge(hi_ready, n)
                    dve.wait_ge(lo_weighed, n - PROBS)
                    dve.tensor_tensor(probs_lo[:, t % PROBS, :], probs[:, t % PROBS, :], probs_hi[:, t % PROBS, :],
                                      ALU.subtract).then_inc(lo_odd_ready, 1)
            take_output(PAIRS - 1)
            normalise(PAIRS)
            take_transposed(PAIRS)
            add_output(PAIRS)
            dve.wait_ge(x_added, PAIRS + 1)

            layernorm(xs, 2)
            transposed(kv_b[0], 2)
            dve.wait_ge(sproj_ready, 1)
            dve.wait_ge(consts, ALL_CONSTS)
            dve.tensor_tensor(sk_blocks[:, :, :], repeated(max_b[0][:, 0:N], SH8),
                              head_rows[:, :].rearrange("p (h a) -> p h a", a=1).broadcast_to([P, SH8, N]),
                              ALU.mult).then_inc(sproj_taken, 1)
            dve.memset(sv[:, :, SHD:SHD + 1], 1.0).then_inc(sproj_taken, 1)
            dve.wait_ge(sproj_ready, 3)
            dve.tensor_copy(sv[:, :, 0:SHD], max_b[1][:, 0:NQ * SHD].rearrange("p (h n) -> p h n", h=NQ)).then_inc(sproj_taken, 1)

            def negative_maxima(f):
                heads, keys = fill_shape(f)
                dve.wait_ge(s_scores, f + 1)
                link(dve.tensor_reduce(smax[:, f, 0:heads], bank[f % 3][:, :].rearrange("p (h k) -> p h k", h=heads),
                                       AX_X, ALU.max))
                dve.tensor_scalar(sneg[:, f, 0:heads], smax[:, f, 0:heads], -1.0, None, ALU.mult).then_inc(s_neg, 1)

            def take_transposes(f):
                dve.wait_ge(s_pt, f + 1)
                dve.tensor_copy(spt_of(f), bank[3 + f % 2][:, :]).then_inc(s_pt_taken, 1)

            for f in range(12 + 2):
                if f < 12:
                    negative_maxima(f)
                if f >= 2:
                    take_transposes(f - 2)
            dve.wait_ge(s_pv, 12)
            for h in range(NQ):
                o = bank[6 + h][:, 0:HEADS * (SHD + 1)].rearrange("p (g n) -> p g n", n=SHD + 1)
                link(dve.reciprocal(sinv[:, h, :], o[:, :, SHD]))
                dve.tensor_tensor(sy[:, h, :].rearrange("p (g n) -> p g n", n=SHD), o[:, :, 0:SHD],
                                  sinv[:, h, :].rearrange("p (g a) -> p g a", a=1).broadcast_to([P, HEADS, SHD]),
                                  ALU.mult).then_inc(sy_ready, 1)
            dve.wait_ge(yt_psum, 1)
            dve.tensor_copy(yt[:, :, :].rearrange("p c n -> p (c n)"), bank[0][:, :]).then_inc(yt_ready, 1)
            dve.wait_ge(sproj_out, 1)
            link(dve.tensor_tensor(xs[:, :, :].rearrange("p h d -> p (h d)"), bank[1][:, :],
                                   xs[:, :, :].rearrange("p h d -> p (h d)"), ALU.add))

            layernorm(xs, 3)
            transposed(bank[2], 3)
            dve.wait_ge(router_ready, 1)
            for h in range(NQ):
                link(dve.tensor_tensor(logits[:, h, :], bank[3][:, h * E:(h + 1) * E], router_b_sb[:, :], ALU.add))
                link(dve.max(top8[:, h, :], logits[:, h, :]))
                link(dve.max_index(top_at[:, h, :], top8[:, h, :], logits[:, h, :]))
            link(dve.tensor_copy(top_no[:, :, :], top_at[:, :, 0:2]))
            dve.tensor_tensor(gap[:, :], top8[:, :, 1], top8[:, :, 0], ALU.subtract).then_inc(gap_ready, 1)
            dve.wait_ge(gap_exp, 1)
            link(dve.tensor_scalar(e_gap1[:, :], e_gap[:, :], 1.0, None, ALU.add))
            link(dve.reciprocal(gate12[:, :, 0], e_gap1[:, :]))
            link(dve.tensor_tensor(gate12[:, :, 1], gate12[:, :, 0], e_gap[:, :], ALU.mult))
            for h in range(NQ):
                link(dve.tensor_scalar(first_gate[:, h, :], expert_no[:, :], top_no[:, h, 0:1], gate12[:, h, 0:1],
                                       ALU.is_equal, ALU.mult))
                link(dve.tensor_scalar(second_gate[:, h, :], expert_no[:, :], top_no[:, h, 1:2], gate12[:, h, 1:2],
                                       ALU.is_equal, ALU.mult))
                link(dve.tensor_tensor(gates[:, h, :], first_gate[:, h, :], second_gate[:, h, :], ALU.add))

            def gate_up(e):
                dve.wait_ge(silu_ready, e + 1)
                dve.tensor_tensor(gated(e), bank[e % 3][:, N:2 * N], act_h[:, e % 2, :], ALU.mult).then_inc(gated_ready, 1)

            def add_expert(e):
                dve.wait_ge(expert_out, e + 1)
                for h in range(NQ):
                    o = bank[3 + e % 2][:, h * D:(h + 1) * D]
                    if e < E:
                        ins = dve.scalar_tensor_tensor(xs[:, h, :], o, gates[:, h, e:e + 1], xs[:, h, :], ALU.mult, ALU.add)
                    else:
                        ins = dve.tensor_tensor(xs[:, h, :], o, xs[:, h, :], ALU.add)
                ins.then_inc(expert_added, 1)
                dve.wait_ge(expert_added, e + 1)

            for e in range(EA + 1):
                if e < EA:
                    gate_up(e)
                if e >= 1:
                    add_expert(e - 1)
            

        @block.tensor
        def _(pe):
            def transposes(to, src, ready, count, done):
                pe.wait_ge(ready, count)
                for c in range(DC):
                    for h in range(NQ):
                        ins = pe.transpose(to[:, c * N + h * P:c * N + (h + 1) * P], src[:, h, c * P:(c + 1) * P], ident[:, :])
                ins.then_inc(done, 1)

            pe.wait_ge(consts, IDENT_CONSTS)
            transposes(out_b[0], xn, xn_ready, 2, xt_psum)

            def wait_values(groups, pairs=0):
                pe.wait_ge(v_hi_ready, pairs * GROUPS + groups)
                pe.wait_ge(v_lo_ready, pairs * GROUPS + groups)

            def queries(n, former=True):
                pe.wait_ge(q_loaded, n * 16 + 16)
                if former:
                    pe.wait_ge(x_added, n)
                    wait_values(0, n)
                else:
                    pe.wait_ge(xt_ready, 1)
                for c in range(DC):
                    ins = pe.matmul(kv_b[1][:, 0:N], q_raw[:, c, :], xt[:, c, :], start=(c == 0), stop=(c == DC - 1))
                ins.then_inc(q_ready, 1)

            def five(main, tail):
                return ((kv_hi, main, ctx_hi), (kv_hi, main, ctx_lo), (kv_lo, main, ctx_hi),
                        (kv_hi, tail, ctx_st), (kv_lo, tail, ctx_st))

            def keys(n, c, former=True):
                if c == 0:
                    pe.wait_ge(w_split, n * 2 + 2)
                if not former:
                    wait_ctx_split(pe, c // 2)
                if c >= 2:
                    pe.wait_ge(k_lo_ready, n * CHUNKS + c - 1)
                elif c == 1:
                    pe.wait_ge(q_taken, n * 2 + 2)
                for s, (w, at, data) in enumerate(five(0, P)):
                    ins = pe.matmul(kv_b[c % 2][:, :], w[:, at:at + P], data[:, tokens(CHUNK * c, CHUNK)],
                                    start=(s == 0), stop=(s == 4))
                ins.then_inc(kv_ready, 1)

            def values(n, g):
                if g < 2:
                    pe.wait_ge(k_lo_ready, n * CHUNKS + CHUNKS - 1 + g)
                else:
                    wait_values(g - 1, n)
                for j in range(GROUP):
                    for s, (w, at, data) in enumerate(five(2 * P, 3 * P)):
                        ins = pe.matmul(kv_b[g % 2][:, j * P:(j + 1) * P], data[:, tokens(P * (GROUP * g + j), P)],
                                        w[:, at:at + P], start=(s == 0), stop=(s == 4))
                ins.then_inc(kv_ready, 1)

            def max_scores(n, j, former=True):
                h, a, c = j % 2, (j // 2) % 2, j // 4
                if a == 0 and h == 0:
                    pe.wait_ge(k_hi_ready, n * CHUNKS + c + 1)
                if j == 0:
                    pe.wait_ge(q_taken, n * 2 + 1)
                if j >= 2 or former:
                    pe.wait_ge(max_taken, n * MAXES + j - 1)
                r = slice(HD * a, HD * a + HD)
                pe.matmul(max_b[j % 2][:, :], q_nat[r, 0, h * P:(h + 1) * P], k_hi[r, tokens(CHUNK * c, CHUNK)],
                          start=True, stop=True).then_inc(max_ready, 1)

            def max_rows(n):
                pe.wait_ge(neg_max_ready, n + 1)
                pe.wait_ge(q_taken, n * 2 + 2)
                for a, row in ((0, HD), (1, 0)):
                    for h in range(NQ):
                        ins = pe.matmul(max_b[0][row:row + 1, h * P:(h + 1) * P], neg_max[:, a * 2 + h:a * 2 + h + 1],
                                        ident_h[:, :], start=True, stop=True)
                ins.then_inc(rows_ready, 1)

            def prepare(n, t, weigh_former=None):
                former = weigh_former is not None
                maxes = MAX_STEP <= t < MAX_STEP + MAXES // 2
                if t == Q_STEP:
                    queries(n, former)
                if maxes:
                    max_scores(n, 2 * (t - MAX_STEP), former)
                if K_STEP <= t < K_STEP + CHUNKS:
                    keys(n, t - K_STEP, former)
                if V_STEP <= t < V_STEP + 2 * (GROUPS - 2) and (t - V_STEP) % 2 == 0:
                    values(n, (t - V_STEP) // 2)
                if former:
                    weigh_former()
                if maxes:
                    max_scores(n, 2 * (t - MAX_STEP) + 1, former)
                if t == ROWS_STEP:
                    max_rows(n)

            def scores(p, t, first=False, last=False):
                if not first or t >= 2:
                    pe.wait_ge(probs_ready if last and t - 2 >= HEAD else hi_ready, p * TILES + t - 1)
                if t % 8 == 0:
                    pe.wait_ge(restacked[t // 8], p * 96 + 96)
                if t == 0:
                    pe.wait_ge(q_stacked, p * 6 + 6)
                sl = tokens(P * t, P)
                for k, (one, two) in enumerate(((A1, A2), (B1, B2))):
                    o = score_b[t % 2][:, k * N:(k + 1) * N]
                    pe.matmul(o, k_st[:, one, sl], q_st[:, one, :], start=True, stop=False)
                    ins = pe.matmul(o, k_st[:, two, sl], q_st[:, two, :], start=False, stop=True)
                ins.then_inc(scores_ready, 1)

            def weigh_hi(p, t, first=False):
                pe.wait_ge(hi_ready, p * TILES + t + 1)
                if t % GROUP == 0:
                    wait_values(t // GROUP + 1, p)
                if t == 0 and not first:
                    pe.wait_ge(out_taken, 2 * p)
                for a in range(2):
                    for h in range(NQ):
                        at = a * N + h * P
                        ins = pe.matmul(out_b[a][:, h * O_COLS:(h + 1) * O_COLS], probs_hi[:, t % PROBS, at:at + P],
                                        v[:, t, a, 0:O_COLS], start=(t == 0 and h == 0), stop=False)
                ins.then_inc(hi_weighed, 1)

            def weigh_lo(p, t, last=False):
                wait_lo(pe, p, t, last)
                for a in range(2):
                    for h in range(NQ):
                        at = a * N + h * P
                        ins = pe.matmul(out_b[a][:, h * O_COLS + HD:(h + 1) * O_COLS],
                                        probs_lo[:, t % PROBS, at:at + P], v[:, t, a, HD:O_COLS],
                                        start=False, stop=(t == TILES - 1 and h == NQ - 1))
                ins.then_inc(lo_weighed, 1)

            def transpose_output(p, last_values):
                pe.wait_ge(o_norm_ready, p)
                wait_values(0, last_values)
                for h in range(NQ):
                    ins = pe.transpose(kv_b[1][:, h * P:(h + 1) * P], o_norm[:, h, :, :].rearrange("p a n -> p (a n)"),
                                       ident[:, :])
                ins.then_inc(o_transposed, 1)

            def project_output(p):
                pe.wait_ge(o_norm_t_ready, p)
                pe.wait_ge(o_loaded, p * 16)
                for h in range(NQ):
                    ins = pe.matmul(kv_b[0][:, h * D:(h + 1) * D], o_norm_t[:, h * P:(h + 1) * P], o_raw[:, :],
                                    start=True, stop=True)
                ins.then_inc(wo_ready, 1)

            for t in range(HEAD, TILES):
                prepare(0, t)
            values(0, GROUPS - 2)
            values(0, GROUPS - 1)
            for t in range(HEAD):
                scores(0, t, True)
                if t >= HI_LAG:
                    weigh_hi(0, t - HI_LAG, True)
                if t >= LO_LAG:
                    weigh_lo(0, t - LO_LAG)

            def weigh(p, t, last=False):
                weigh_hi(p, t - HI_LAG)
                weigh_lo(p, t - LO_LAG, last)

            with pe.Fori(0, PAIRS - 1) as i:
                for t in range(HEAD, TILES):
                    scores(i, t)
                    prepare(i + 1, t, lambda: weigh(i, t))
                values(i + 1, GROUPS - 2)
                weigh_hi(i, TILES - 2)
                weigh_lo(i, TILES - 4)
                values(i + 1, GROUPS - 1)
                weigh_lo(i, TILES - 3)
                for t in range(HEAD):
                    scores(i + 1, t)
                    if t == 0:
                        weigh_hi(i, TILES - 1)
                        weigh_lo(i, TILES - 2)
                    if t == 1:
                        weigh_lo(i, TILES - 1)
                    if t == 4:
                        transpose_output(i + 1, i + 2)
                    if t == 6:
                        project_output(i + 1)
                    if t >= HI_LAG:
                        weigh_hi(i + 1, t - HI_LAG)
                    if t >= LO_LAG:
                        weigh_lo(i + 1, t - LO_LAG)
            for t in range(HEAD, TILES):
                scores(PAIRS - 1, t, last=True)
                weigh(PAIRS - 1, t, True)
            weigh_hi(PAIRS - 1, TILES - 2)
            weigh_hi(PAIRS - 1, TILES - 1)
            for t in range(TILES - LO_LAG, TILES):
                weigh_lo(PAIRS - 1, t, True)
            transpose_output(PAIRS, PAIRS)
            project_output(PAIRS)

            transposes(kv_b[0], xn, xn_ready, 4, xt_psum)
            pe.wait_ge(xt_ready, 2)
            pe.wait_ge(w_tail_loaded, 16 * 8)
            pe.wait_ge(consts, ALL_CONSTS)
            for c in range(DC):
                ins = pe.matmul(max_b[0][:, 0:N], w_sk_sb[:, c, :], xt[:, c, :], start=(c == 0), stop=(c == DC - 1))
            ins.then_inc(sproj_ready, 1)
            for f in range(DC):
                for c in range(DC):
                    ins = pe.matmul(kv_b[1][:, f * N:(f + 1) * N], w_sq_sb[:, c, f * P:(f + 1) * P], xt[:, c, :],
                                    start=(c == 0), stop=(c == DC - 1))
            ins.then_inc(sproj_ready, 1)
            for h in range(NQ):
                for c in range(DC):
                    ins = pe.matmul(max_b[1][:, h * SHD:(h + 1) * SHD], xt[:, c, h * P:(h + 1) * P], w_sv_sb[:, c, :],
                                    start=(c == 0), stop=(c == DC - 1))
            ins.then_inc(sproj_ready, 1)
            pe.wait_ge(sq_taken, 1)
            pe.wait_ge(sproj_taken, 3)

            def self_scores(f):
                c, tile = f // 6, 0 if f % 6 < 2 else 1
                heads, nk = fill_shape(f)
                h0 = heads * (f % 6 - (0 if tile == 0 else 2))
                if f >= 3:
                    pe.wait_ge(s_exp, f - 2)
                pe.matmul(bank[f % 3][:, :], sq[:, c, tile * P:(tile + 1) * P], sk_blocks[:, h0:h0 + heads, 0:nk],
                          start=True, stop=False)
                diagonal = bank[f % 3][:, :].rearrange("p (h k) -> p h k", h=heads)[:, :, nk - P:nk]
                pe.matmul(diagonal, ident_b[:, :], diag4[:, 0:heads, :], start=False, stop=True).then_inc(s_scores, 1)

            def self_transposes(f):
                pe.wait_ge(s_exp, f + 1)
                if f >= 2:
                    pe.wait_ge(s_pt_taken, f - 1)
                for b in range(4):
                    ins = pe.transpose(bank[3 + f % 2][:, b * P:(b + 1) * P], sp[:, f, b * P:(b + 1) * P], ident[:, :])
                ins.then_inc(s_pt, 1)

            def self_weigh(f):
                c, tile = f // 6, 0 if f % 6 < 2 else 1
                heads, nk = fill_shape(f)
                h0 = SH8 * c + heads * (f % 6 - (0 if tile == 0 else 2))
                pe.wait_ge(s_pt_taken, f + 1)
                for h in range(heads):
                    o = bank[6 + tile][:, (h0 + h) * (SHD + 1):(h0 + h + 1) * (SHD + 1)]
                    for k in range(nk // P):
                        b = h * (nk // P) + k
                        ins = pe.matmul(o, spt_of(f)[:, b * P:(b + 1) * P], sv[:, k, :], start=(k == 0), stop=(k == nk // P - 1))
                ins.then_inc(s_pv, 1)

            for f in range(12 + 3):
                if f < 12:
                    self_scores(f)
                if 1 <= f < 13:
                    self_transposes(f - 1)
                if f >= 3:
                    self_weigh(f - 3)
            transposes(bank[0], sy, sy_ready, 2, yt_psum)
            pe.wait_ge(yt_ready, 1)
            for h in range(NQ):
                for c in range(DC):
                    ins = pe.matmul(bank[1][:, h * D:(h + 1) * D], yt[:, c, h * P:(h + 1) * P], w_proj_sb[:, c, :],
                                    start=(c == 0), stop=(c == DC - 1))
            ins.then_inc(sproj_out, 1)

            transposes(bank[2], xn, xn_ready, 6, xt_psum)
            pe.wait_ge(xt_ready, 3)
            pe.wait_ge(w2_loaded, 16)
            for e in range(EA + 1):
                if e < EA:
                    if e >= 3:
                        pe.wait_ge(gated_ready, e - 2)
                    for k, w in enumerate((w1_sb, w3_sb)):
                        for c in range(DC):
                            ins = pe.matmul(bank[e % 3][:, k * N:(k + 1) * N], w[:, e, c, :], xt[:, c, :],
                                            start=(c == 0), stop=(c == DC - 1))
                    ins.then_inc(h_ready, 1)
                if e == 0:
                    for h in range(NQ):
                        for c in range(DC):
                            ins = pe.matmul(bank[3][:, h * E:(h + 1) * E], xt[:, c, h * P:(h + 1) * P],
                                            router_w_sb[:, c, :], start=(c == 0), stop=(c == DC - 1))
                    ins.then_inc(router_ready, 1)
                if e >= 1:
                    d = e - 1
                    pe.wait_ge(gated_ready, d + 1)
                    if d == 0:
                        pe.wait_ge(gap_ready, 1)
                    for h in range(NQ):
                        if d >= 2 and h == 0:
                            pe.wait_ge(expert_added, d - 1)
                        ins = pe.matmul(bank[3 + d % 2][:, h * D:(h + 1) * D], gated(d)[:, h * P:(h + 1) * P], w2_sb[:, d, :],
                                        start=True, stop=True)
                    ins.then_inc(expert_out, 1)


def kernel(**inputs):
    import concourse.bacc as _bacc
    from concourse import mybir as _mybir
    from concourse.bass_utils import run_bass_kernel_spmd as _run

    a = {k: np.asarray(v) for k, v in inputs.items()}

    def by_pair(w):
        w = w.reshape(w.shape[0], PAIRS, P).transpose(1, 0, 2)
        return np.concatenate([w, w[-1:]], axis=0)

    wk, wv = by_pair(a["L0_xattn_Wk"]), by_pair(a["L0_xattn_Wv"])
    w_attn = a["L0_attn_w_attn"]
    arrays = {
        "x": a["x"][0],
        "ctx_main": a["ctx_768"][0].T[0:P],
        "ctx_tail": a["ctx_768"][0].T[P:CD],
        "w_kv": np.concatenate([part for w in (wk, wv) for part in (w[:, 0:P], np.concatenate([w[:, P:CD]] * 2, axis=1))], axis=2),
        "w_q": by_pair(a["L0_xattn_Wq"]).reshape(PAIRS + 1, DC, P, P).transpose(0, 2, 1, 3),
        "w_o": a["L0_xattn_Wo"].reshape(PAIRS, P, D),
        "bo": a["L0_xattn_bo"],
        "w_sq": w_attn[:, 0:D],
        "w_sk": np.concatenate([w_attn[:, D:D + SHD]] * SH8, axis=1),
        "w_sv": w_attn[:, D + SHD:D + 2 * SHD],
        "w_proj": a["L0_attn_w_proj"],
        "router_w": a["L0_ffn_router_w"],
        "router_b": a["L0_ffn_router_b"],
        "w1": np.concatenate([a["L0_ffn_routed_w1"], a["L0_ffn_shared_w1"]], axis=0),
        "w3": np.concatenate([a["L0_ffn_routed_w3"], a["L0_ffn_shared_w3"]], axis=0),
        "w2": np.concatenate([a["L0_ffn_routed_w2"], a["L0_ffn_shared_w2"]], axis=0),
    }
    arrays = {f"in_{k}": np.ascontiguousarray(v) for k, v in arrays.items()}
    nc = _bacc.Bacc("TRN2", target_bir_lowering=False, num_devices=1)
    args = [nc.dram_tensor(k, v.shape, _mybir.dt.from_np(v.dtype), kind="ExternalInput").ap() for k, v in arrays.items()]
    out = nc.dram_tensor("out", (N, D), F32, kind="ExternalOutput").ap()
    build(nc, *args, out)
    r = _run(nc, [arrays], core_ids=[0])
    return r.results[0]["out"].reshape(1, N, D)
```

```python
from contextlib import ExitStack

import concourse.bass as bass
import numpy as np
from concourse import mybir

F32 = mybir.dt.float32
F16 = mybir.dt.float16
BF16 = mybir.dt.bfloat16
U32 = mybir.dt.uint32
ALU = mybir.AluOpType
ACT = mybir.ActivationFunctionType
AX_X = mybir.AxisListType.X

P = 128
N = 256
NQ = N // P
D = 256
DC = D // P
M = 4096
CD = 192
HEADS = 16
HD = 64
PAIRS = HEADS // 2
TILES = M // P
CHUNK = 512
CHUNKS = M // CHUNK
GROUP = 4
GROUPS = TILES // GROUP
RESTACK = 1024
RESTACKS = M // RESTACK
PROBS = 8
W_SCALE = 256.0
MAX_UNIT = 64.0
Q_SCALE = float(HD) ** -0.5
EPS = 1e-5

SHD = 16
SH8 = P // SHD
S_SCALE = float(SHD) ** -0.5
MASKED = -1e30
FILLS_0, FILLS = 4, 12
E = 8
ES = 2
EA = E + ES
H = 128
TE = NQ * EA

HEAD = 8
Q_STEP = 8
K_STEP = 9
MAX_STEP = 11
V_STEPS = (17, 19, 21, 23, 25, 28)
V_STEPS_FIRST = (17, 18, 19, 21, 24, 27, 28, 30)
CTX_STEPS = (9, 11, 14)
M4_STEP = 27
ROWS_STEP = 29
MAXES = 2 * NQ * CHUNKS
IDENT_CONSTS, ZERO_CONSTS, QK_CONSTS, ALL_CONSTS = 6, 8, 10, 19
MAX_UNITS = float(np.array([MAX_UNIT] * 2, np.float16).view(np.float32)[0])
DVE_HI = (3, 5)
HI_LAG, LO_LAG = 2, 4
O_COLS = 2 * HD + 1
V_COLS = O_COLS + 1
P_SCALE = 64.0
POOL_K, POOL_V = 3, 7
COPIES = 4
A1, B1, A2, B2 = range(4)


def build(nc, x, ctx_main, ctx_tail, w_kv, w_q, w_o, bo, w_sq, w_sk, w_sv, w_proj, router_w,
          router_b, w1, w3, w2, out):
    with ExitStack() as stack:
        def sb(name, shape, dt):
            return stack.enter_context(nc.sbuf_tensor(name, shape, dt))

        def sem(name):
            return stack.enter_context(nc.semaphore(name))

        ctx_hi = sb("ctx_hi", [P, M], F16)
        ctx_lo = sb("ctx_lo", [P, M], F16)
        ctx_st = sb("ctx_st", [P, M], F16)
        k_hi = sb("k_hi", [P, M], F16)
        k_lo = sb("k_lo", [P, M], F16)
        k_st = sb("k_st", [P, 4, M], F16)
        v = sb("v", [P, TILES, 2, V_COLS], F16)
        v_f32 = v[:, :, :, :].rearrange("p t a n -> p (t a n)").bitcast(F32)
        probs = sb("probs", [P, PROBS, 2 * N], F32)
        probs_hi = sb("probs_hi", [P, PROBS, 2 * N], F16)
        probs_lo = sb("probs_lo", [P, PROBS, 2 * N], F16)
        kv_raw = sb("kv_raw", [P, 4 * P], F32)
        kv_hi = sb("kv_hi", [P, 4 * P], F16)
        kv_lo = sb("kv_lo", [P, 4 * P], F16)
        q_raw = sb("q_raw", [P, DC, P], F32)
        o_raw = sb("o_raw", [P, D], F32)
        q_nat = sb("q_nat", [P, 2, N], F16)
        q_st = sb("q_st", [P, 4, N], F16)
        max_part = sb("max_part", [P, 2 * NQ, CHUNKS], F32)
        max4 = sb("max4", [P, 2 * NQ], F32)
        neg_max = sb("neg_max", [P, 2 * NQ], F16)
        o_parts = sb("o_parts", [P, 2, NQ, O_COLS], F32)
        inv_sum = sb("inv_sum", [P, 2, NQ, 1], F32)
        o_both = sb("o_both", [P, 2, NQ, HD], F32)
        o_norm = sb("o_norm", [P, NQ, 2, HD], F32)
        o_norm_t = sb("o_norm_t", [P, N], F32)
        ident = sb("ident", [P, P], F32)
        ident_h = sb("ident_h", [P, P], F16)
        ident_b = sb("ident_b", [P, P], BF16)
        xs = sb("xs", [P, NQ, D], F32)
        x_in = sb("x_in", [P, NQ, D], F32)
        bo_all = sb("bo_all", [P, D], F32)
        xn = sb("xn", [P, NQ, D], F32)
        xt = sb("xt", [P, DC, N], F32)
        stats = sb("stats", [P, NQ, 6], F32)
        mean_var = sb("mean_var", [P, NQ, 2], F32)
        std = sb("std", [P, NQ], F32)
        inv_std = sb("inv_std", [P, NQ], F32)
        w_sq_sb = sb("w_sq_sb", [P, DC, D], F32)
        w_sk_sb = sb("w_sk_sb", [P, DC, P], F32)
        w_sv_sb = sb("w_sv_sb", [P, DC, SHD], F32)
        w_proj_sb = sb("w_proj_sb", [P, DC, D], F32)
        head_rows = sb("head_rows", [P, SH8], F32)
        diag4 = sb("diag4", [P, 4, P], BF16)
        sq = sb("sq", [P, DC, N], F32)
        sv_hi = sb("sv_hi", [P, NQ, SHD + 1], F16)
        sv_lo = sb("sv_lo", [P, NQ, SHD + 1], F16)
        smax = sb("smax", [P, FILLS, 4], F32)
        sneg = sb("sneg", [P, FILLS, 4], F32)
        sinv = sb("sinv", [P, NQ, HEADS], F32)
        sy = sb("sy", [P, NQ, D], F32)
        k_st_f32 = k_st[:, :, :].rearrange("p a m -> p (a m)").bitcast(F32)
        sp = k_st_f32[:, 0:FILLS * 512].rearrange("p (f n) -> p f n", n=512)
        sk_blocks = k_st_f32[:, FILLS * 512:16 * 512].rearrange("p (h n) -> p h n", h=SH8)
        v_flat = v[:, :, :, :].rearrange("p t a n -> p (t a n)")
        yt = sb("yt", [P, DC, N], F32)
        router_w_sb = sb("router_w_sb", [P, DC, E], F32)
        router_b_sb = sb("router_b_sb", [P, E], F32)
        expert_no = sb("expert_no", [P, E], F32)
        logits = sb("logits", [P, NQ, E], F32)
        top8 = sb("top8", [P, NQ, 8], F32)
        top_at = sb("top_at", [P, NQ, 8], U32)
        top_no = sb("top_no", [P, NQ, 2], F32)
        gap = sb("gap", [P, NQ], F32)
        e_gap = sb("e_gap", [P, NQ], F32)
        e_gap1 = sb("e_gap1", [P, NQ], F32)
        gate12 = sb("gate12", [P, NQ, 2], F32)
        first_gate = sb("first_gate", [P, NQ, E], F32)
        second_gate = sb("second_gate", [P, NQ, E], F32)
        gates = sb("gates", [P, NQ, E], F32)
        w1_sb = sb("w1_sb", [P, EA, DC, H], F32)
        w3_sb = sb("w3_sb", [P, EA, DC, H], F32)
        w2_sb = sb("w2_sb", [P, EA, D], F32)
        act_h = sb("act_h", [P, 2, P], F32)
        minus_half = sb("minus_half", [P, 1], F32)
        base_e = sb("base_e", [P, 1], F32)

        bank = [stack.enter_context(nc.psum_tensor(f"bank{i}", [P, 512], F32)) for i in range(8)]
        score_b = bank[0:2]
        out_b = (bank[2], bank[7])
        kv_b = bank[3:5]
        max_b = bank[5:7]

        x_loaded, bo_loaded, w_tail_loaded = sem("x_loaded"), sem("bo_loaded"), sem("w_tail_loaded")
        w2_loaded = sem("w2_loaded")
        ctx_loaded = [sem(f"ctx_loaded{i}") for i in range(RESTACKS)]
        kv_loaded, q_loaded, o_loaded = sem("kv_loaded"), sem("q_loaded"), sem("o_loaded")
        restacked = [sem(f"restacked{i}") for i in range(RESTACKS)]
        ctx_hi_ready, ctx_lo_ready, ctx_pool_lo = sem("ctx_hi_ready"), sem("ctx_lo_ready"), sem("ctx_pool_lo")
        consts = sem("consts")
        w_split = sem("w_split")
        q_ready, q_taken = sem("q_ready"), sem("q_taken")
        kv_ready = sem("kv_ready")
        k_hi_ready, k_lo_ready = sem("k_hi_ready"), sem("k_lo_ready")
        v_hi_ready, v_lo_ready = sem("v_hi_ready"), sem("v_lo_ready")
        max_ready, max_taken = sem("max_ready"), sem("max_taken")
        max4_ready, neg_max_ready = sem("max4_ready"), sem("neg_max_ready")
        rows_ready = sem("rows_ready")
        q_stacked = sem("q_stacked")
        scores_ready, probs_ready = sem("scores_ready"), sem("probs_ready")
        hi_ready, lo_ready = sem("hi_ready"), sem("lo_ready")
        lo_odd_ready = sem("lo_odd_ready")
        hi_weighed, lo_weighed = sem("hi_weighed"), sem("lo_weighed")
        out_taken, o_chain = sem("out_taken"), sem("o_chain")
        o_transposed, o_norm_t_ready = sem("o_transposed"), sem("o_norm_t_ready")
        copied = sem("copied")
        o_norm_ready, wo_ready, x_added = sem("o_norm_ready"), sem("wo_ready"), sem("x_added")
        var_ready, std_ready, xn_ready = sem("var_ready"), sem("std_ready"), sem("xn_ready")
        xt_psum, xt_ready = sem("xt_psum"), sem("xt_ready")
        sproj_ready, sproj_taken, sq_taken = sem("sproj_ready"), sem("sproj_taken"), sem("sq_taken")
        sk_ready = sem("sk_ready")
        s_scores, s_neg, s_exp = sem("s_scores"), sem("s_neg"), sem("s_exp")
        s_pt, s_pt_hi, s_pt_lo, s_pv = sem("s_pt"), sem("s_pt_hi"), sem("s_pt_lo"), sem("s_pv")
        sy_ready, yt_psum, yt_ready, sproj_out = sem("sy_ready"), sem("yt_psum"), sem("yt_ready"), sem("sproj_out")
        var_tile_ready, inv_std_ready = sem("var_tile_ready"), sem("inv_std_ready")
        xt3_psum, xt3_ready = sem("xt3_psum"), sem("xt3_ready")
        router_ready, gap_ready, gap_exp = sem("router_ready"), sem("gap_ready"), sem("gap_exp")
        h_ready, silu_ready, gated_ready = sem("h_ready"), sem("silu_ready"), sem("gated_ready")
        expert_out, expert_added = sem("expert_out"), sem("expert_added")
        dve_step = sem("dve_step")
        stored = sem("stored")

        block = stack.enter_context(nc.Block())

        def v_part(g, at):
            return v[:, GROUP * g:GROUP * (g + 1), :, at:at + HD].rearrange("p t a n -> p (t a) n")

        def kv_group(g):
            return kv_b[g % 2][:, :].rearrange("p (t n) -> p t n", n=HD)

        def raw_chunk(j):
            if j < 2:
                flat = probs[:, :, :].rearrange("p b n -> p (b n)")
            else:
                flat = v_f32
            at = (j % 2) * 2 * RESTACK
            return flat[:, at:at + RESTACK], flat[:, at + RESTACK:at + 2 * RESTACK]

        def wait_ctx_split(engine, j):
            engine.wait_ge(ctx_hi_ready, 2 * (j + 1))
            engine.wait_ge(ctx_lo_ready, j + 2)
            if j > 0:
                engine.wait_ge(ctx_pool_lo, j)

        def max_banks(former):
            return (*max_b,) if former else (*max_b, *score_b)

        def copy_buffer(m):
            return probs[:, PROBS - COPIES + m % COPIES, :]

        def wait_copy_used(engine, m):
            if m < CHUNKS - POOL_K:
                engine.wait_ge(k_lo_ready, POOL_K + m + 1)
            else:
                engine.wait_ge(v_lo_ready, POOL_K + m - CHUNKS + 1)

        def wait_lo(engine, p, t, last):
            if not last or t < HEAD:
                engine.wait_ge(lo_ready, p * TILES + t + 1)
            elif t % 2 == 0:
                engine.wait_ge(lo_ready, p * TILES + HEAD + (t - HEAD) // 2 + 1)
            else:
                engine.wait_ge(lo_odd_ready, (t - HEAD) // 2 + 1)

        def tokens(first, count):
            return slice(first, first + count)

        last_wo_b = (kv_b[0], out_b[0])

        def fill(f):
            if f < FILLS_0:
                return f // 2, 0, 4 * (f % 2), 4, P
            f -= FILLS_0
            return f // 4, 1, 2 * (f % 4), 2, 2 * P

        def gated(e):
            return ctx_hi[:, :].bitcast(F32)[:, (e % 16) * P:(e % 16 + 1) * P]

        def spt_of(f):
            if f < 8:
                both = v_flat[:, f * 1024:(f + 1) * 1024]
            else:
                both = (k_hi, k_lo)[(f - 8) // 2][:, ((f - 8) % 2) * 1024:((f - 8) % 2 + 1) * 1024]
            return both[:, 0:512], both[:, 512:1024]

        def repeated(ap, n):
            return ap.rearrange("p (a m) -> p a m", a=1).broadcast_to([ap.shape[0], n, ap.shape[1]])

        @block.sync
        def _(sp_q):
            sp_q.dma_start(x_in[:, :, :], x.rearrange("(h p) d -> p h d", p=P)).then_inc(x_loaded, 16)
            sp_q.dma_start(kv_raw[:, :], w_kv[0]).then_inc(kv_loaded, 16)

            def load_ctx(j):
                sl = tokens(RESTACK * j, RESTACK)
                main, tail = raw_chunk(j)
                sp_q.dma_start(main, ctx_main[:, sl]).then_inc(ctx_loaded[j], 16)
                sp_q.dma_start(tail[0:HD, :], ctx_tail[:, sl]).then_inc(ctx_loaded[j], 16)
                sp_q.dma_start(tail[HD:P, :], ctx_tail[:, sl]).then_inc(ctx_loaded[j], 16)

            load_ctx(0)
            sp_q.dma_start(q_raw[:, :, :], w_q[0]).then_inc(q_loaded, 16)
            load_ctx(1)
            sp_q.dma_start(bo_all[:, :], bo.rearrange("(a d) -> a d", a=1).broadcast_to([P, D])).then_inc(bo_loaded, 16)
            load_ctx(2)
            load_ctx(3)
            sp_q.wait_ge(w_split, 2)
            sp_q.dma_start(kv_raw[:, :], w_kv[1]).then_inc(kv_loaded, 16)
            sp_q.wait_ge(q_ready, 1)
            sp_q.dma_start(q_raw[:, :, :], w_q[1]).then_inc(q_loaded, 16)

            def restack(g, parts, former_scores=None):
                sp_q.wait_ge(k_lo_ready, parts)
                sp_q.wait_ge(k_hi_ready, parts)
                if former_scores is not None:
                    sp_q.wait_ge(scores_ready, former_scores)
                sl = tokens(RESTACK * g, RESTACK)
                for rows, to, which, part in (
                    (slice(0, HD), slice(0, HD), A1, k_hi), (slice(0, HD), slice(0, HD), A2, k_hi),
                    (slice(HD, P), slice(HD, P), B1, k_hi), (slice(HD, P), slice(HD, P), B2, k_hi),
                    (slice(0, HD), slice(HD, P), A1, k_lo), (slice(HD, P), slice(0, HD), B1, k_lo),
                ):
                    sp_q.dma_start(k_st[to, which, sl], part[rows, sl]).then_inc(restacked[g], 16)

            sp_q.wait_ge(consts, ZERO_CONSTS)
            for g in range(RESTACKS):
                restack(g, 2 * (g + 1))
            for to, frm in (
                (w_sq_sb[:, :, :], w_sq.rearrange("(c p) n -> p c n", p=P)),
                (w_sk_sb[:, :, :], w_sk.rearrange("(c p) n -> p c n", p=P)),
                (w_sv_sb[:, :, :], w_sv.rearrange("(c p) n -> p c n", p=P)),
                (w_proj_sb[:, :, :], w_proj.rearrange("(c p) n -> p c n", p=P)),
                (router_w_sb[:, :, :], router_w.rearrange("(c p) n -> p c n", p=P)),
                (router_b_sb[:, :], router_b.rearrange("(a d) -> a d", a=1).broadcast_to([P, E])),
                (w1_sb[:, :, :, :], w1.rearrange("e (c p) h -> p e c h", p=P)),
                (w3_sb[:, :, :, :], w3.rearrange("e (c p) h -> p e c h", p=P)),
            ):
                sp_q.dma_start(to, frm).then_inc(w_tail_loaded, 16)
            sp_q.dma_start(w2_sb[:, :, :], w2.rearrange("e h d -> h e d")).then_inc(w2_loaded, 16)

            with sp_q.Fori(0, PAIRS - 1) as i:
                def now(value):
                    return sp_q.snap(sp_q.to_reg(value))

                after_next = now(i + 2)
                split = now(i * 2 + 4)
                parts = [now((i + 1) * CHUNKS + 2 * (g + 1)) for g in range(RESTACKS)]
                former = [now(i * TILES + 8 * (g + 1)) for g in range(RESTACKS)]
                w_o_i = w_o[bass.ds(i, 1), :, :].rearrange("a p d -> (a p) d")
                w_kv_i = w_kv[bass.ds(after_next, 1), :, :].rearrange("a p d -> (a p) d")
                w_q_i = w_q[bass.ds(after_next, 1), :, :, :].rearrange("a p c d -> (a p) c d")
                sp_q.wait_ge(x_added, i + 1)
                sp_q.dma_start(o_raw[:, :], w_o_i).then_inc(o_loaded, 16)
                sp_q.wait_ge(w_split, split)
                sp_q.dma_start(kv_raw[:, :], w_kv_i).then_inc(kv_loaded, 16)
                sp_q.wait_ge(q_ready, after_next)
                sp_q.dma_start(q_raw[:, :, :], w_q_i).then_inc(q_loaded, 16)
                for g in range(RESTACKS):
                    restack(g, parts[g], former[g])
            sp_q.wait_ge(wo_ready, PAIRS - 1)
            sp_q.dma_start(o_raw[:, :], w_o[PAIRS - 1]).then_inc(o_loaded, 16)
            sp_q.wait_ge(kv_loaded, 16 * (PAIRS + 1))
            sp_q.wait_ge(q_loaded, 16 * (PAIRS + 1))

            for h in range(NQ):
                sp_q.wait_ge(expert_added, EA * (h + 1))
                sp_q.dma_start(out[h * P:(h + 1) * P, :], xs[:, h, :]).then_inc(stored, 16)
            sp_q.wait_ge(stored, 16 * NQ)

        @block.gpsimd
        def _(pool):
            made = [0]

            def const(ins):
                made[0] += 1
                ins.then_inc(consts, 1)
                pool.wait_ge(consts, made[0])

            for m in (ident, ident_h, ident_b):
                const(pool.memset(m[:, :], 0.0))
                const(pool.affine_select(out=m[:, :], in_=m[:, :], compare_op=ALU.not_equal, fill=1.0, base=0,
                                         pattern=[[-1, P]], channel_multiplier=1))
            const(pool.memset(k_st[:, A2:B2 + 1, :].rearrange("p a m -> p (a m)").bitcast(F32), 0.0))
            const(pool.memset(q_st[:, A2:B2 + 1, :], 0.0))
            const(pool.memset(k_st[HD:HD + 1, A2, :].bitcast(F32), MAX_UNITS))
            const(pool.memset(k_st[0:1, B2, :].bitcast(F32), MAX_UNITS))
            for j in range(1, RESTACKS):
                sl = tokens(RESTACK * j, RESTACK)
                _, tail = raw_chunk(j)
                pool.wait_ge(ctx_loaded[j], 48)
                pool.wait_ge(ctx_hi_ready, 2 * j + 2)
                pool.tensor_tensor(ctx_st[HD:P, sl], tail[HD:P, :], ctx_st[HD:P, sl],
                                   ALU.subtract).then_inc(ctx_pool_lo, 1)
                pool.wait_ge(ctx_pool_lo, j)
                if j == 2:
                    const(pool.memset(diag4[:, :, :], 0.0))
                    const(pool.affine_select(out=diag4[:, :, :], in_=diag4[:, :, :], compare_op=ALU.is_ge,
                                             fill=MASKED, base=0, pattern=[[0, 4], [-1, P]], channel_multiplier=1))
            const(pool.memset(head_rows[:, :], 1.0))
            const(pool.affine_select(out=head_rows[:, :], in_=head_rows[:, :], compare_op=ALU.is_ge,
                                     fill=0.0, base=0, pattern=[[-SHD, SH8]], channel_multiplier=1))
            const(pool.affine_select(out=head_rows[:, :], in_=head_rows[:, :], compare_op=ALU.is_ge,
                                     fill=0.0, base=SHD - 1, pattern=[[SHD, SH8]], channel_multiplier=-1))
            const(pool.iota(expert_no[:, :], pattern=[[1, E]], base=0, channel_multiplier=0,
                            allow_small_or_imprecise_dtypes=True))
            const(pool.memset(minus_half[:, :], -0.5))
            const(pool.memset(base_e[:, :], float(np.e)))
            wait_ctx_split(pool, RESTACKS - 1)
            const(pool.memset(v[:, :, :, 2 * HD:2 * HD + 1], 1.0))
            for m in range(CHUNKS - POOL_K + POOL_V):
                c, g = POOL_K + m, POOL_K + m - CHUNKS
                pool.wait_ge(copied, m + 1)
                if g < 0:
                    pool.wait_ge(k_lo_ready, c)
                    sl = tokens(CHUNK * c, CHUNK)
                    pool.tensor_tensor(k_lo[:, sl], copy_buffer(m), k_hi[:, sl], ALU.subtract).then_inc(k_lo_ready, 1)
                    pool.wait_ge(k_lo_ready, c + 1)
                else:
                    pool.tensor_tensor(v_part(g, 0), copy_buffer(m).rearrange("p (t n) -> p t n", n=HD), v_part(g, HD),
                                       ALU.subtract).then_inc(v_lo_ready, 1)
                    pool.wait_ge(v_lo_ready, g + 1)
            def step(p, t, first=False):
                pool.wait_ge(hi_ready, p * TILES + t + 1)
                if not first:
                    pool.wait_ge(lo_weighed, p * TILES + t + 1 - PROBS)
                pool.tensor_tensor(probs_lo[:, t % PROBS, :], probs[:, t % PROBS, :], probs_hi[:, t % PROBS, :],
                                   ALU.subtract).then_inc(lo_ready, 1)

            for t in range(HEAD):
                step(0, t, True)
            with pool.Fori(0, PAIRS - 1) as i:
                for t in range(HEAD, TILES):
                    step(i, t)
                for t in range(HEAD):
                    step(i + 1, t)
            for t in range(HEAD, TILES, 2):
                step(PAIRS - 1, t)

            def inverse_std(h, count):
                pool.wait_ge(var_tile_ready, count)
                pool.tensor_tensor(inv_std[:, h:h + 1], mean_var[:, h, 1:2], minus_half[:, :],
                                   ALU.pow).then_inc(inv_std_ready, 1)

            for h in range(NQ):
                inverse_std(h, h + 1)
            for h in range(NQ):
                inverse_std(h, NQ + h + 1)
                pool.wait_ge(gap_ready, h + 1)
                pool.tensor_tensor(e_gap[:, h:h + 1], base_e[:, :], gap[:, h:h + 1], ALU.pow).then_inc(gap_exp, 1)

        @block.scalar
        def _(act):
            act.wait_ge(var_ready, 1)
            act.activation(std[:, :], mean_var[:, :, 1], ACT.Sqrt).then_inc(std_ready, 1)
            act.wait_ge(std_ready, 1)
            act.activation(e_gap[:, :], std[:, :], ACT.Exp)

            def split_ctx(j):
                act.wait_ge(ctx_loaded[j], 48)
                sl = tokens(RESTACK * j, RESTACK)
                main, tail = raw_chunk(j)
                act.copy(ctx_hi[:, sl], main).then_inc(ctx_hi_ready, 1)
                act.copy(ctx_st[:, sl], tail).then_inc(ctx_hi_ready, 1)

            def step(p, t, first=False, last=False):
                act.wait_ge(scores_ready, p * TILES + t + 1)
                if not first:
                    wait_lo(act, p, t - PROBS, last)
                act.activation(probs[:, t % PROBS, :], score_b[t % 2][:, :], ACT.Exp).then_inc(probs_ready, 1)
                if last or (not first and t in DVE_HI):
                    return
                if not first:
                    act.wait_ge(hi_weighed, p * TILES + t + 1 - PROBS)
                    if t - 1 in DVE_HI:
                        act.wait_ge(hi_ready, p * TILES + t)
                act.activation(probs_hi[:, t % PROBS, :], score_b[t % 2][:, :], ACT.Exp).then_inc(hi_ready, 1)

            def copy(m, psum):
                if m == 0:
                    wait_ctx_split(act, 1)
                if m >= COPIES:
                    wait_copy_used(act, m - COPIES)
                act.activation(copy_buffer(m), psum[:, :], ACT.Copy, scale=1.0 / W_SCALE).then_inc(copied, 1)

            def prepare(n, t, former=True):
                if K_STEP <= t < K_STEP + CHUNKS:
                    c = t - K_STEP
                    act.wait_ge(kv_ready, n * (CHUNKS + GROUPS) + c + 1)
                    if former:
                        act.wait_ge(restacked[c // 2], n * 96)
                        act.wait_ge(max_ready, n * MAXES)
                    act.activation(k_hi[:, tokens(CHUNK * c, CHUNK)], kv_b[c % 2][:, :], ACT.Copy,
                                   scale=1.0 / W_SCALE).then_inc(k_hi_ready, 1)
                    if not former and c >= POOL_K:
                        copy(c - POOL_K, kv_b[c % 2])
                steps = V_STEPS if former else V_STEPS_FIRST
                if t in steps:
                    values(n, steps.index(t), former)

            def values(n, g, former=True):
                act.wait_ge(kv_ready, n * (CHUNKS + GROUPS) + CHUNKS + g + 1)
                if former:
                    act.wait_ge(lo_weighed, (n - 1) * TILES + GROUP * (g + 1))
                elif g == 0:
                    wait_ctx_split(act, RESTACKS - 1)
                act.activation(v_part(g, HD), kv_group(g), ACT.Copy, scale=1.0 / W_SCALE).then_inc(v_hi_ready, 1)
                if not former and g < POOL_V:
                    copy(CHUNKS - POOL_K + g, kv_b[g % 2])

            split_ctx(0)
            split_ctx(1)
            for t in range(HEAD, TILES):
                prepare(0, t, False)
                if t in (K_STEP + 1, K_STEP + 2):
                    split_ctx(t - K_STEP + 1)
            for t in range(HEAD):
                if t == PROBS - COPIES:
                    act.wait_ge(v_lo_ready, POOL_V)
                step(0, t, True)
            with act.Fori(0, PAIRS - 1) as i:
                for t in range(HEAD, TILES):
                    step(i, t)
                    prepare(i + 1, t)
                values(i + 1, GROUPS - 2)
                for t in range(HEAD):
                    step(i + 1, t)
                    if t == 3:
                        values(i + 1, GROUPS - 1)
            for t in range(HEAD, TILES):
                step(PAIRS - 1, t, last=True)

            def take_queries(c, psum, made):
                act.wait_ge(sproj_ready, made)
                act.activation(sq[:, c, :], psum[:, 0:N], ACT.Copy, scale=S_SCALE).then_inc(sq_taken, 1)

            take_queries(0, kv_b[1], 2)
            for f in range(FILLS + 2):
                if f >= 2:
                    act.wait_ge(s_pt, f - 1)
                    act.copy(spt_of(f - 2)[0], bank[3 + f % 2][:, :]).then_inc(s_pt_hi, 1)
                if f < FILLS:
                    _, _, _, heads, keys = fill(f)
                    act.wait_ge(s_neg, f + 1)
                    for h in range(heads):
                        last = act.activation(sp[:, f, h * keys:(h + 1) * keys],
                                              bank[f % 3][:, h * keys:(h + 1) * keys], ACT.Exp,
                                              bias=sneg[:, f, h:h + 1])
                    last.then_inc(s_exp, 1)
                if f == 1:
                    take_queries(1, bank[2], 3)
            for s in range(TE):
                act.wait_ge(h_ready, s + 1)
                if s >= 2:
                    act.wait_ge(gated_ready, s - 1)
                act.activation(act_h[:, s % 2, :], bank[s % 3][:, 0:P], ACT.Silu).then_inc(silu_ready, 1)

        @block.vector
        def _(dve):
            chain = [0]

            def link(ins):
                chain[0] += 1
                ins.then_inc(dve_step, 1)
                dve.wait_ge(dve_step, chain[0])

            def split_weights(n, former=True):
                dve.wait_ge(kv_loaded, n * 16 + 16)
                if former:
                    dve.wait_ge(kv_ready, n * (CHUNKS + GROUPS))
                dve.tensor_scalar(kv_hi[:, :], kv_raw[:, :], W_SCALE, None, ALU.mult).then_inc(w_split, 1)
                dve.wait_ge(w_split, n * 2 + 1)
                dve.scalar_tensor_tensor(kv_lo[:, :], kv_raw[:, :], W_SCALE, kv_hi[:, :],
                                         ALU.mult, ALU.subtract).then_inc(w_split, 1)

            dve.wait_ge(x_loaded, 16)
            for h in range(NQ):
                link(dve.bn_stats(stats[:, h, :], x_in[:, h, :]))
                link(dve.bn_aggr(mean_var[:, h, :], stats[:, h, :]))
            dve.tensor_scalar(mean_var[:, :, 1], mean_var[:, :, 1], EPS, None, ALU.add).then_inc(var_ready, 1)
            dve.wait_ge(std_ready, 1)
            link(dve.reciprocal(inv_std[:, :], std[:, :]))
            for h in range(NQ):
                dve.tensor_scalar(xn[:, h, :], x_in[:, h, :], mean_var[:, h, 0:1], inv_std[:, h:h + 1],
                                  ALU.subtract, ALU.mult).then_inc(xn_ready, 1)
            split_weights(0, False)
            dve.wait_ge(xt_psum, 1)
            dve.tensor_copy(xt[:, :, :].rearrange("p c n -> p (c n)"), out_b[0][:, :]).then_inc(xt_ready, 1)

            def split_ctx(j):
                sl = tokens(RESTACK * j, RESTACK)
                dve.wait_ge(ctx_loaded[j], 48)
                dve.wait_ge(ctx_hi_ready, 2 * j + 1)
                main, tail = raw_chunk(j)
                dve.tensor_tensor(ctx_lo[:, sl], main, ctx_hi[:, sl], ALU.subtract).then_inc(ctx_lo_ready, 1)
                if j == 0:
                    dve.wait_ge(ctx_hi_ready, 2)
                    dve.tensor_tensor(ctx_st[HD:P, sl], tail[HD:P, :], ctx_st[HD:P, sl],
                                      ALU.subtract).then_inc(ctx_lo_ready, 1)

            def split_queries(n, former=True):
                dve.wait_ge(q_ready, n + 1)
                if former:
                    dve.wait_ge(max_ready, n * MAXES)
                    dve.wait_ge(q_stacked, n * 6)
                dve.tensor_scalar(q_nat[:, 0, :], kv_b[1][:, 0:N], Q_SCALE, None, ALU.mult).then_inc(q_taken, 1)
                dve.wait_ge(q_taken, n * 2 + 1)
                dve.scalar_tensor_tensor(q_nat[:, 1, :], kv_b[1][:, 0:N], Q_SCALE, q_nat[:, 0, :],
                                         ALU.mult, ALU.subtract).then_inc(q_taken, 1)

            def prepare(n, t, former=True):
                if t == Q_STEP:
                    split_weights(n, former)
                    split_queries(n, former)
                def part_max(j):
                    dve.wait_ge(max_ready, n * MAXES + j + 1)
                    if former and j == 0:
                        dve.wait_ge(max4_ready, n)
                    banks = max_banks(former)
                    dve.tensor_reduce(max_part[:, j % 4, j // 4:j // 4 + 1], banks[j % len(banks)][:, :], AX_X,
                                      ALU.max).then_inc(max_taken, 1)

                maxes = MAX_STEP <= t < MAX_STEP + MAXES // 2
                if maxes:
                    part_max(2 * (t - MAX_STEP))
                if maxes and not former:
                    part_max(2 * (t - MAX_STEP) + 1)
                if K_STEP <= t < K_STEP + (CHUNKS if former else POOL_K):
                    c = t - K_STEP
                    sl = tokens(CHUNK * c, CHUNK)
                    dve.wait_ge(k_hi_ready, n * CHUNKS + c + 1)
                    if former:
                        dve.wait_ge(restacked[c // 2], n * 96)
                    dve.scalar_tensor_tensor(k_lo[:, sl], kv_b[c % 2][:, :], 1.0 / W_SCALE, k_hi[:, sl],
                                             ALU.mult, ALU.subtract).then_inc(k_lo_ready, 1)
                if former and t - 1 in V_STEPS:
                    values(n, V_STEPS.index(t - 1))
                if maxes and former:
                    part_max(2 * (t - MAX_STEP) + 1)
                if t == M4_STEP:
                    dve.wait_ge(max_taken, n * MAXES + MAXES)
                    if former:
                        dve.wait_ge(neg_max_ready, n)
                        dve.wait_ge(rows_ready, n)
                    dve.tensor_reduce(max4[:, :], max_part[:, :, :], AX_X, ALU.max).then_inc(max4_ready, 1)
                    dve.wait_ge(max4_ready, n + 1)
                    dve.tensor_scalar(neg_max[:, :], max4[:, :], -1.0 / MAX_UNIT, float(np.log(P_SCALE)) / MAX_UNIT,
                                      ALU.mult, ALU.add).then_inc(neg_max_ready, 1)

            def values(n, g):
                dve.wait_ge(v_hi_ready, n * GROUPS + g + 1)
                dve.scalar_tensor_tensor(v_part(g, 0), kv_group(g), 1.0 / W_SCALE, v_part(g, HD),
                                         ALU.mult, ALU.subtract).then_inc(v_lo_ready, 1)

            def stack_queries(n, former=True):
                if former:
                    dve.wait_ge(scores_ready, n * TILES)
                dve.wait_ge(q_taken, n * 2 + 2)
                dve.tensor_copy(q_st[0:HD, A1:B2 + 1:2, :], q_nat[0:HD, :, :]).then_inc(q_stacked, 1)
                dve.tensor_copy(q_st[HD:P, B1:B2 + 1:2, :], q_nat[HD:P, :, :]).then_inc(q_stacked, 1)
                dve.tensor_copy(q_st[HD:P, A1, :], q_nat[0:HD, 0, :]).then_inc(q_stacked, 1)
                dve.tensor_copy(q_st[0:HD, B1, :], q_nat[HD:P, 0, :]).then_inc(q_stacked, 1)
                dve.wait_ge(rows_ready, n + 1)
                dve.tensor_copy(q_st[HD:HD + 1, A2, :], max_b[0][HD:HD + 1, 0:N]).then_inc(q_stacked, 1)
                dve.tensor_copy(q_st[0:1, B2, :], max_b[0][0:1, 0:N]).then_inc(q_stacked, 1)

            def take_output(p):
                dve.wait_ge(lo_weighed, p * TILES + TILES)
                dve.wait_ge(x_added, p + 1)
                for a in range(2):
                    dve.tensor_copy(o_parts[:, a, :, :].rearrange("p h n -> p (h n)"),
                                    out_b[a][:, 0:NQ * O_COLS]).then_inc(out_taken, 1)

            def normalise(p):
                dve.wait_ge(out_taken, 2 * p)
                dve.reciprocal(inv_sum[:, :, :, :], o_parts[:, :, :, 2 * HD:2 * HD + 1]).then_inc(o_chain, 1)
                dve.tensor_tensor(o_both[:, :, :, :], o_parts[:, :, :, HD:2 * HD], o_parts[:, :, :, 0:HD],
                                  ALU.add).then_inc(o_chain, 1)
                dve.wait_ge(o_chain, 2 * p)
                dve.wait_ge(x_added, p)
                for a in range(2):
                    ins = dve.tensor_tensor(o_norm[:, :, a, :], o_both[:, a, :, :],
                                            inv_sum[:, a, :, :].broadcast_to([P, NQ, HD]), ALU.mult)
                ins.then_inc(o_norm_ready, 1)

            def take_transposed(p):
                dve.wait_ge(o_transposed, p)
                dve.tensor_copy(o_norm_t[:, :], kv_b[0][:, 0:N]).then_inc(o_norm_t_ready, 1)

            def add_output(p):
                dve.wait_ge(wo_ready, p)
                dve.wait_ge(x_added, p)
                dve.tensor_tensor(xs[:, :, :].rearrange("p h d -> p (h d)"), kv_b[1][:, :],
                                  xs[:, :, :].rearrange("p h d -> p (h d)"), ALU.add).then_inc(x_added, 1)

            def finish(p, t):
                if t in DVE_HI:
                    dve.wait_ge(probs_ready, p * TILES + t + 1)
                    dve.wait_ge(hi_ready, p * TILES + t)
                    dve.wait_ge(hi_weighed, p * TILES + t + 1 - PROBS)
                    dve.wait_ge(lo_ready, p * TILES + t + 1 - PROBS)
                    dve.tensor_copy(probs_hi[:, t % PROBS, :], probs[:, t % PROBS, :]).then_inc(hi_ready, 1)
                if t == 2:
                    normalise(p)
                if t == 4:
                    take_transposed(p)
                    values(p, GROUPS - 1)
                if t == 6:
                    add_output(p)

            split_ctx(0)
            split_queries(0, False)
            for t in range(K_STEP, TILES):
                if t in CTX_STEPS:
                    split_ctx(CTX_STEPS.index(t) + 1)
                prepare(0, t, False)
            dve.wait_ge(consts, QK_CONSTS)
            stack_queries(0, False)
            dve.wait_ge(v_lo_ready, POOL_V)
            for g in range(POOL_V, GROUPS):
                values(0, g)
            dve.wait_ge(bo_loaded, 16)
            for h in range(NQ):
                ins = dve.tensor_tensor(xs[:, h, :], x_in[:, h, :], bo_all[:, :], ALU.add)
            ins.then_inc(x_added, 1)
            with dve.Fori(0, PAIRS - 1) as i:
                for t in range(HEAD, TILES):
                    prepare(i + 1, t)
                stack_queries(i + 1)
                values(i + 1, GROUPS - 2)
                take_output(i)
                for t in range(HEAD):
                    finish(i + 1, t)
            for t in range(HEAD, TILES):
                n = (PAIRS - 1) * TILES + t + 1
                dve.wait_ge(probs_ready, n)
                dve.wait_ge(hi_weighed, n - PROBS)
                wait_lo(dve, PAIRS - 1, t - PROBS, True)
                dve.tensor_copy(probs_hi[:, t % PROBS, :], probs[:, t % PROBS, :]).then_inc(hi_ready, 1)
                if t % 2 == 1:
                    dve.wait_ge(hi_ready, n)
                    dve.wait_ge(lo_weighed, n - PROBS)
                    dve.tensor_tensor(probs_lo[:, t % PROBS, :], probs[:, t % PROBS, :], probs_hi[:, t % PROBS, :],
                                      ALU.subtract).then_inc(lo_odd_ready, 1)
            take_output(PAIRS - 1)
            normalise(PAIRS)
            take_transposed(PAIRS)

            def add_and_measure(h, psum):
                link(dve.tensor_tensor(xs[:, h, :], psum[:, 0:D], xs[:, h, :], ALU.add))
                link(dve.bn_stats(stats[:, h, :], xs[:, h, :]))
                link(dve.bn_aggr(mean_var[:, h, :], stats[:, h, :]))
                dve.tensor_scalar(mean_var[:, h, 1:2], mean_var[:, h, 1:2], EPS, None,
                                  ALU.add).then_inc(var_tile_ready, 1)

            def normalise_tile(h, count):
                dve.wait_ge(inv_std_ready, count)
                dve.tensor_scalar(xn[:, h, :], xs[:, h, :], mean_var[:, h, 0:1], inv_std[:, h:h + 1],
                                  ALU.subtract, ALU.mult).then_inc(xn_ready, 1)

            def take_tile(to, h, psum, psum_ready, count, taken):
                dve.wait_ge(psum_ready, count)
                dve.tensor_copy(to[:, :, h * P:(h + 1) * P],
                                psum[:, 0:DC * P].rearrange("p (c n) -> p c n", c=DC)).then_inc(taken, 1)

            dve.wait_ge(x_added, PAIRS)
            for h in range(NQ):
                dve.wait_ge(wo_ready, PAIRS + h)
                add_and_measure(h, last_wo_b[h])
            for h in range(NQ):
                normalise_tile(h, h + 1)
            for h in range(NQ):
                take_tile(xt, h, bank[h], xt_psum, 2 + h, xt_ready)

            dve.wait_ge(sproj_ready, 1)
            dve.wait_ge(consts, ALL_CONSTS)
            for h0, h1, k0, k1 in ((0, SH8 // 2, 0, P), (SH8 // 2, SH8, 0, P), (0, SH8, P, N)):
                dve.tensor_tensor(sk_blocks[:, h0:h1, k0:k1], repeated(max_b[0][:, k0:k1], h1 - h0),
                                  head_rows[:, h0:h1].rearrange("p (h a) -> p h a", a=1).broadcast_to([P, h1 - h0, k1 - k0]),
                                  ALU.mult).then_inc(sk_ready, 1)
            dve.memset(sv_hi[:, :, SHD:SHD + 1], 1.0)
            dve.memset(sv_lo[:, :, SHD:SHD + 1], 0.0).then_inc(sproj_taken, 1)
            def take_values():
                dve.wait_ge(sproj_ready, 4)
                sv_psum = max_b[1][:, 0:NQ * SHD].rearrange("p (h n) -> p h n", h=NQ)
                link(dve.tensor_copy(sv_hi[:, :, 0:SHD], sv_psum))
                dve.tensor_tensor(sv_lo[:, :, 0:SHD], sv_psum, sv_hi[:, :, 0:SHD], ALU.subtract).then_inc(sproj_taken, 1)

            def negative_maxima(f):
                heads = fill(f)[3]
                dve.wait_ge(s_scores, f + 1)
                link(dve.tensor_reduce(smax[:, f, 0:heads], bank[f % 3][:, :].rearrange("p (h k) -> p h k", h=heads),
                                       AX_X, ALU.max))
                dve.tensor_scalar(sneg[:, f, 0:heads], smax[:, f, 0:heads], -1.0, float(np.log(P_SCALE)),
                                  ALU.mult, ALU.add).then_inc(s_neg, 1)

            def take_transposes(f):
                hi, lo = spt_of(f)
                dve.wait_ge(s_pt_hi, f + 1)
                dve.tensor_tensor(lo, bank[3 + f % 2][:, :], hi, ALU.subtract).then_inc(s_pt_lo, 1)

            def head_outputs(h):
                dve.wait_ge(s_pv, (FILLS_0, FILLS)[h])
                o = bank[6 + h][:, 0:HEADS * (SHD + 1)].rearrange("p (g n) -> p g n", n=SHD + 1)
                link(dve.reciprocal(sinv[:, h, :], o[:, :, SHD]))
                dve.tensor_tensor(sy[:, h, :].rearrange("p (g n) -> p g n", n=SHD), o[:, :, 0:SHD],
                                  sinv[:, h, :].rearrange("p (g a) -> p g a", a=1).broadcast_to([P, HEADS, SHD]),
                                  ALU.mult).then_inc(sy_ready, 1)

            def top_two(h):
                dve.wait_ge(router_ready, h + 1)
                link(dve.tensor_tensor(logits[:, h, :], bank[6][:, 0:E], router_b_sb[:, :], ALU.add))
                link(dve.max(top8[:, h, :], logits[:, h, :]))
                link(dve.max_index(top_at[:, h, :], top8[:, h, :], logits[:, h, :]))
                dve.tensor_copy(top_no[:, h, :], top_at[:, h, 0:2])
                dve.tensor_tensor(gap[:, h:h + 1], top8[:, h, 1:2], top8[:, h, 0:1], ALU.subtract).then_inc(gap_ready, 1)

            def gate_values(h):
                dve.wait_ge(gap_exp, h + 1)
                link(dve.tensor_scalar(e_gap1[:, h:h + 1], e_gap[:, h:h + 1], 1.0, None, ALU.add))
                link(dve.reciprocal(gate12[:, h, 0:1], e_gap1[:, h:h + 1]))
                link(dve.tensor_tensor(gate12[:, h, 1:2], gate12[:, h, 0:1], e_gap[:, h:h + 1], ALU.mult))

            def spread_gates(h):
                for k, to in enumerate((first_gate, second_gate)):
                    ins = dve.tensor_scalar(to[:, h, :], expert_no[:, :], top_no[:, h, k:k + 1], gate12[:, h, k:k + 1],
                                            ALU.is_equal, ALU.mult)
                link(ins)
                link(dve.tensor_tensor(gates[:, h, :], first_gate[:, h, :], second_gate[:, h, :], ALU.add))

            for f in range(FILLS + 2):
                if f < FILLS:
                    negative_maxima(f)
                if f == 1:
                    take_values()
                if f >= 2:
                    take_transposes(f - 2)
                if f == FILLS_0 + 3:
                    head_outputs(0)
                if f == FILLS_0 + 4:
                    take_tile(yt, 0, bank[5], yt_psum, 1, yt_ready)
                if f == FILLS_0 + 5:
                    dve.wait_ge(sproj_out, 1)
                    add_and_measure(0, bank[5])
                if f == FILLS_0 + 6:
                    normalise_tile(0, NQ + 1)
                if f == FILLS_0 + 7:
                    take_tile(xt, 0, bank[5], xt3_psum, 1, xt3_ready)
            def gate_up(s):
                dve.wait_ge(silu_ready, s + 1)
                dve.tensor_tensor(gated(s), bank[s % 3][:, P:2 * P], act_h[:, s % 2, :], ALU.mult).then_inc(gated_ready, 1)

            def add_expert(s):
                h, e = s // EA, s % EA
                dve.wait_ge(expert_out, s + 1)
                o = bank[3 + s % 2][:, 0:D]
                if e < E:
                    ins = dve.scalar_tensor_tensor(xs[:, h, :], o, gates[:, h, e:e + 1], xs[:, h, :], ALU.mult, ALU.add)
                else:
                    ins = dve.tensor_tensor(xs[:, h, :], o, xs[:, h, :], ALU.add)
                ins.then_inc(expert_added, 1)
                dve.wait_ge(expert_added, s + 1)

            gate_up(0)
            head_outputs(1)
            top_two(0)
            gate_up(1)
            gate_values(0)
            gate_up(2)
            spread_gates(0)
            for s in range(TE):
                add_expert(s)
                if s + 3 < TE:
                    gate_up(s + 3)
                if s == 1:
                    take_tile(yt, 1, bank[5], yt_psum, 2, yt_ready)
                if s == 2:
                    dve.wait_ge(sproj_out, 2)
                    add_and_measure(1, bank[5])
                if s == 3:
                    normalise_tile(1, NQ + 2)
                if s == 4:
                    take_tile(xt, 1, bank[5], xt3_psum, 2, xt3_ready)
                if s == 6:
                    top_two(1)
                if s == 7:
                    gate_values(1)
                if s == 8:
                    spread_gates(1)

        @block.tensor
        def _(pe):
            def transposes(to, src, ready, count, done):
                pe.wait_ge(ready, count)
                for c in range(DC):
                    for h in range(NQ):
                        ins = pe.transpose(to[:, c * N + h * P:c * N + (h + 1) * P], src[:, h, c * P:(c + 1) * P], ident[:, :])
                ins.then_inc(done, 1)

            def keep_warm(products, psum):
                for _ in range(products):
                    pe.matmul(psum[:, 0:P], ident_h[:, :], ident_h[:, :], start=True, stop=True)

            pe.wait_ge(consts, IDENT_CONSTS)
            keep_warm(30, out_b[1])
            transposes(out_b[0], xn, xn_ready, 2, xt_psum)
            keep_warm(12, out_b[1])

            def wait_values(groups, pairs=0):
                pe.wait_ge(v_hi_ready, pairs * GROUPS + groups)
                pe.wait_ge(v_lo_ready, pairs * GROUPS + groups)

            def queries(n, former=True):
                pe.wait_ge(q_loaded, n * 16 + 16)
                if former:
                    pe.wait_ge(x_added, n)
                    wait_values(0, n)
                else:
                    pe.wait_ge(xt_ready, 1)
                for c in range(DC):
                    ins = pe.matmul(kv_b[1][:, 0:N], q_raw[:, c, :], xt[:, c, :], start=(c == 0), stop=(c == DC - 1))
                ins.then_inc(q_ready, 1)

            def five(main, tail):
                return ((kv_hi, main, ctx_hi), (kv_hi, main, ctx_lo), (kv_lo, main, ctx_hi),
                        (kv_hi, tail, ctx_st), (kv_lo, tail, ctx_st))

            def keys(n, c, former=True):
                if c == 0:
                    pe.wait_ge(w_split, n * 2 + 2)
                if not former:
                    wait_ctx_split(pe, c // 2)
                if not former and c >= POOL_K + 2:
                    pe.wait_ge(copied, c - 2 - POOL_K + 1)
                elif c >= 2:
                    pe.wait_ge(k_lo_ready, n * CHUNKS + c - 1)
                elif c == 1:
                    pe.wait_ge(q_taken, n * 2 + 2)
                for s, (w, at, data) in enumerate(five(0, P)):
                    ins = pe.matmul(kv_b[c % 2][:, :], w[:, at:at + P], data[:, tokens(CHUNK * c, CHUNK)],
                                    start=(s == 0), stop=(s == 4))
                ins.then_inc(kv_ready, 1)

            def values(n, g, former=True):
                if not former:
                    pe.wait_ge(copied, CHUNKS - POOL_K + g - 1)
                elif g < 2:
                    pe.wait_ge(k_lo_ready, n * CHUNKS + CHUNKS - 1 + g)
                else:
                    wait_values(g - 1, n)
                for j in range(GROUP):
                    for s, (w, at, data) in enumerate(five(2 * P, 3 * P)):
                        ins = pe.matmul(kv_b[g % 2][:, j * P:(j + 1) * P], data[:, tokens(P * (GROUP * g + j), P)],
                                        w[:, at:at + P], start=(s == 0), stop=(s == 4))
                ins.then_inc(kv_ready, 1)

            def max_scores(n, j, former=True):
                h, a, c = j % 2, (j // 2) % 2, j // 4
                if a == 0 and h == 0:
                    pe.wait_ge(k_hi_ready, n * CHUNKS + c + 1)
                if j == 0:
                    pe.wait_ge(q_taken, n * 2 + 1)
                banks = max_banks(former)
                if j >= len(banks) or former:
                    pe.wait_ge(max_taken, n * MAXES + j - len(banks) + 1)
                r = slice(HD * a, HD * a + HD)
                pe.matmul(banks[j % len(banks)][:, :], q_nat[r, 0, h * P:(h + 1) * P], k_hi[r, tokens(CHUNK * c, CHUNK)],
                          start=True, stop=True).then_inc(max_ready, 1)

            def max_rows(n):
                pe.wait_ge(neg_max_ready, n + 1)
                pe.wait_ge(q_taken, n * 2 + 2)
                for a, row in ((0, HD), (1, 0)):
                    for h in range(NQ):
                        ins = pe.matmul(max_b[0][row:row + 1, h * P:(h + 1) * P], neg_max[:, a * 2 + h:a * 2 + h + 1],
                                        ident_h[:, :], start=True, stop=True)
                ins.then_inc(rows_ready, 1)

            def prepare(n, t, weigh_former=None):
                former = weigh_former is not None
                maxes = MAX_STEP <= t < MAX_STEP + MAXES // 2
                if t == Q_STEP:
                    queries(n, former)
                if maxes:
                    max_scores(n, 2 * (t - MAX_STEP), former)
                    if not former:
                        max_scores(n, 2 * (t - MAX_STEP) + 1, former)
                if K_STEP <= t < K_STEP + CHUNKS:
                    keys(n, t - K_STEP, former)
                steps = V_STEPS if former else V_STEPS_FIRST
                if t in steps:
                    values(n, steps.index(t), former)
                if former:
                    weigh_former()
                    if maxes:
                        max_scores(n, 2 * (t - MAX_STEP) + 1, former)
                if t == ROWS_STEP:
                    max_rows(n)

            def scores(p, t, first=False, last=False):
                if not first or t >= 2:
                    pe.wait_ge(probs_ready if last and t - 2 >= HEAD else hi_ready, p * TILES + t - 1)
                if t % 8 == 0:
                    pe.wait_ge(restacked[t // 8], p * 96 + 96)
                if t == 0:
                    pe.wait_ge(q_stacked, p * 6 + 6)
                sl = tokens(P * t, P)
                for k, (one, two) in enumerate(((A1, A2), (B1, B2))):
                    o = score_b[t % 2][:, k * N:(k + 1) * N]
                    pe.matmul(o, k_st[:, one, sl], q_st[:, one, :], start=True, stop=False)
                    ins = pe.matmul(o, k_st[:, two, sl], q_st[:, two, :], start=False, stop=True)
                ins.then_inc(scores_ready, 1)

            def weigh_hi(p, t, first=False):
                pe.wait_ge(hi_ready, p * TILES + t + 1)
                if t % GROUP == 0:
                    wait_values(t // GROUP + 1, p)
                for a in range(2):
                    if t == 0 and not first:
                        pe.wait_ge(out_taken, 2 * p - 1 + a)
                    for h in range(NQ):
                        at = a * N + h * P
                        ins = pe.matmul(out_b[a][:, h * O_COLS:(h + 1) * O_COLS], probs_hi[:, t % PROBS, at:at + P],
                                        v[:, t, a, 0:O_COLS], start=(t == 0 and h == 0), stop=False)
                ins.then_inc(hi_weighed, 1)

            def weigh_lo(p, t, last=False):
                wait_lo(pe, p, t, last)
                for a in range(2):
                    for h in range(NQ):
                        at = a * N + h * P
                        ins = pe.matmul(out_b[a][:, h * O_COLS + HD:(h + 1) * O_COLS],
                                        probs_lo[:, t % PROBS, at:at + P], v[:, t, a, HD:O_COLS],
                                        start=False, stop=(t == TILES - 1 and h == NQ - 1))
                ins.then_inc(lo_weighed, 1)

            def transpose_output(p, last_values):
                pe.wait_ge(o_norm_ready, p)
                wait_values(-1, last_values)
                for h in range(NQ):
                    ins = pe.transpose(kv_b[0][:, h * P:(h + 1) * P], o_norm[:, h, :, :].rearrange("p a n -> p (a n)"),
                                       ident[:, :])
                ins.then_inc(o_transposed, 1)

            def project_output(p, last_values):
                pe.wait_ge(o_norm_t_ready, p)
                wait_values(0, last_values)
                pe.wait_ge(o_loaded, p * 16)
                for h in range(NQ):
                    ins = pe.matmul(kv_b[1][:, h * D:(h + 1) * D], o_norm_t[:, h * P:(h + 1) * P], o_raw[:, :],
                                    start=True, stop=True)
                ins.then_inc(wo_ready, 1)

            for t in range(HEAD, TILES):
                prepare(0, t)
                if t == Q_STEP:
                    keep_warm(16, out_b[1])
                if t == K_STEP + 1:
                    keep_warm(8, out_b[1])
            for t in range(HEAD):
                scores(0, t, True)
                if t >= HI_LAG:
                    weigh_hi(0, t - HI_LAG, True)
                if t >= LO_LAG:
                    weigh_lo(0, t - LO_LAG)

            def weigh(p, t, last=False):
                weigh_hi(p, t - HI_LAG)
                weigh_lo(p, t - LO_LAG, last)

            with pe.Fori(0, PAIRS - 1) as i:
                for t in range(HEAD, TILES):
                    scores(i, t)
                    prepare(i + 1, t, lambda: weigh(i, t))
                values(i + 1, GROUPS - 2)
                weigh_hi(i, TILES - 2)
                weigh_lo(i, TILES - 4)
                weigh_lo(i, TILES - 3)
                for t in range(HEAD):
                    scores(i + 1, t)
                    if t == 0:
                        weigh_hi(i, TILES - 1)
                        weigh_lo(i, TILES - 2)
                    if t == 1:
                        weigh_lo(i, TILES - 1)
                        values(i + 1, GROUPS - 1)
                    if t == 4:
                        transpose_output(i + 1, i + 2)
                    if t == 6:
                        project_output(i + 1, i + 2)
                    if t >= HI_LAG:
                        weigh_hi(i + 1, t - HI_LAG)
                    if t >= LO_LAG:
                        weigh_lo(i + 1, t - LO_LAG)
            for t in range(HEAD, TILES):
                scores(PAIRS - 1, t, last=True)
                weigh(PAIRS - 1, t, True)
            weigh_hi(PAIRS - 1, TILES - 2)
            weigh_hi(PAIRS - 1, TILES - 1)
            for t in range(TILES - LO_LAG, TILES):
                weigh_lo(PAIRS - 1, t, True)
            keep_warm(34, max_b[1])
            transpose_output(PAIRS, PAIRS)
            keep_warm(12, max_b[1])
            pe.wait_ge(o_norm_t_ready, PAIRS)
            pe.wait_ge(o_loaded, PAIRS * 16)
            for h in range(NQ):
                pe.matmul(last_wo_b[h][:, 0:D], o_norm_t[:, h * P:(h + 1) * P], o_raw[:, :],
                          start=True, stop=True).then_inc(wo_ready, 1)

            def tile_transposes(psum, src, h, ready, count, done):
                pe.wait_ge(ready, count)
                for c in range(DC):
                    ins = pe.transpose(psum[:, c * P:(c + 1) * P], src[:, h, c * P:(c + 1) * P], ident[:, :])
                ins.then_inc(done, 1)

            keep_warm(36, max_b[1])
            for h in range(NQ):
                tile_transposes(bank[h], xn, h, xn_ready, 3 + h, xt_psum)
            keep_warm(10, max_b[1])
            pe.wait_ge(xt_ready, 3)
            pe.wait_ge(w_tail_loaded, 16 * 8)
            pe.wait_ge(consts, ALL_CONSTS)
            for c in range(DC):
                ins = pe.matmul(max_b[0][:, 0:N], w_sk_sb[:, c, :], xt[:, c, :], start=(c == 0), stop=(c == DC - 1))
            ins.then_inc(sproj_ready, 1)

            def self_queries(f, psum):
                for c in range(DC):
                    ins = pe.matmul(psum[:, 0:N], w_sq_sb[:, c, f * P:(f + 1) * P], xt[:, c, :],
                                    start=(c == 0), stop=(c == DC - 1))
                ins.then_inc(sproj_ready, 1)

            def self_values():
                for h in range(NQ):
                    for c in range(DC):
                        ins = pe.matmul(max_b[1][:, h * SHD:(h + 1) * SHD], xt[:, c, h * P:(h + 1) * P],
                                        w_sv_sb[:, c, :], start=(c == 0), stop=(c == DC - 1))
                ins.then_inc(sproj_ready, 1)

            self_queries(0, kv_b[1])

            def self_scores(f):
                c, tile, h0, heads, nk = fill(f)
                pe.wait_ge(sk_ready, min(f + 1, 2) if tile == 0 else 3)
                pe.wait_ge(sq_taken, c + 1)
                if f >= 3:
                    pe.wait_ge(s_exp, f - 2)
                pe.matmul(bank[f % 3][:, :], sq[:, c, tile * P:(tile + 1) * P], sk_blocks[:, h0:h0 + heads, 0:nk],
                          start=True, stop=False)
                diagonal = bank[f % 3][:, :].rearrange("p (h k) -> p h k", h=heads)[:, :, nk - P:nk]
                pe.matmul(diagonal, ident_b[:, :], diag4[:, 0:heads, :], start=False, stop=True).then_inc(s_scores, 1)

            def self_transposes(f):
                pe.wait_ge(s_exp, f + 1)
                if f >= 2:
                    pe.wait_ge(s_pt_lo, f - 1)
                for b in range(4):
                    ins = pe.transpose(bank[3 + f % 2][:, b * P:(b + 1) * P], sp[:, f, b * P:(b + 1) * P], ident[:, :])
                ins.then_inc(s_pt, 1)

            def self_weigh(f):
                c, tile, h0, heads, nk = fill(f)
                hi, lo = spt_of(f)
                pe.wait_ge(s_pt_lo, f + 1)
                pe.wait_ge(sproj_taken, 2)
                for h in range(heads):
                    at = (SH8 * c + h0 + h) * (SHD + 1)
                    o = bank[6 + tile][:, at:at + SHD + 1]
                    products = [(part, k, values_part) for k in range(nk // P)
                                for part, values_part in ((hi, sv_hi), (hi, sv_lo), (lo, sv_hi))]
                    for m, (part, k, values_part) in enumerate(products):
                        b = h * (nk // P) + k
                        ins = pe.matmul(o, part[:, b * P:(b + 1) * P], values_part[:, k, :],
                                        start=(m == 0), stop=(m == len(products) - 1))
                ins.then_inc(s_pv, 1)

            def self_project(h):
                pe.wait_ge(yt_ready, h + 1)
                for c in range(DC):
                    ins = pe.matmul(bank[5][:, 0:D], yt[:, c, h * P:(h + 1) * P], w_proj_sb[:, c, :],
                                    start=(c == 0), stop=(c == DC - 1))
                ins.then_inc(sproj_out, 1)

            def route(h):
                pe.wait_ge(xt3_ready, h + 1)
                if h == 1:
                    pe.wait_ge(gap_ready, 1)
                for c in range(DC):
                    ins = pe.matmul(bank[6][:, 0:E], xt[:, c, h * P:(h + 1) * P], router_w_sb[:, c, :],
                                    start=(c == 0), stop=(c == DC - 1))
                ins.then_inc(router_ready, 1)

            def expert_up(s):
                h, e = s // EA, s % EA
                if s < 3:
                    pe.wait_ge(s_exp, FILLS - 2 + s)
                else:
                    pe.wait_ge(gated_ready, s - 2)
                if e == 0:
                    pe.wait_ge(xt3_ready, h + 1)
                for k, w in enumerate((w1_sb, w3_sb)):
                    for c in range(DC):
                        ins = pe.matmul(bank[s % 3][:, k * P:(k + 1) * P], w[:, e, c, :], xt[:, c, h * P:(h + 1) * P],
                                        start=(c == 0), stop=(c == DC - 1))
                ins.then_inc(h_ready, 1)

            def expert_down(s):
                pe.wait_ge(gated_ready, s + 1)
                if s >= 2:
                    pe.wait_ge(expert_added, s - 1)
                pe.matmul(bank[3 + s % 2][:, 0:D], gated(s), w2_sb[:, s % EA, :],
                          start=True, stop=True).then_inc(expert_out, 1)

            for f in range(FILLS + 3):
                if f < FILLS:
                    self_scores(f)
                if f == 1:
                    self_queries(1, bank[2])
                    self_values()
                if f >= 3:
                    self_weigh(f - 3)
                if 1 <= f <= FILLS:
                    self_transposes(f - 1)
                if f == FILLS_0 + 4:
                    tile_transposes(bank[5], sy, 0, sy_ready, 1, yt_psum)
                if f == FILLS_0 + 5:
                    self_project(0)
                if f == FILLS_0 + 7:
                    tile_transposes(bank[5], xn, 0, xn_ready, 5, xt3_psum)
                if f == FILLS:
                    pe.wait_ge(w2_loaded, 16)
                    route(0)
                if f >= FILLS:
                    expert_up(f - FILLS)
            for s in range(TE):
                expert_down(s)
                if s + 3 < TE:
                    expert_up(s + 3)
                if s == 1:
                    tile_transposes(bank[5], sy, 1, sy_ready, 2, yt_psum)
                if s == 2:
                    self_project(1)
                if s == 4:
                    tile_transposes(bank[5], xn, 1, xn_ready, 6, xt3_psum)
                if s == 6:
                    route(1)


def kernel(**inputs):
    import concourse.bacc as _bacc
    from concourse import mybir as _mybir
    from concourse.bass_utils import run_bass_kernel_spmd as _run

    a = {k: np.asarray(v) for k, v in inputs.items()}

    def by_pair(w):
        w = w.reshape(w.shape[0], PAIRS, P).transpose(1, 0, 2)
        return np.concatenate([w, w[-1:]], axis=0)

    wk, wv = by_pair(a["L0_xattn_Wk"]), by_pair(a["L0_xattn_Wv"])
    w_attn = a["L0_attn_w_attn"]
    arrays = {
        "x": a["x"][0],
        "ctx_main": a["ctx_768"][0].T[0:P],
        "ctx_tail": a["ctx_768"][0].T[P:CD],
        "w_kv": np.concatenate([part for w in (wk, wv) for part in (w[:, 0:P], np.concatenate([w[:, P:CD]] * 2, axis=1))], axis=2),
        "w_q": by_pair(a["L0_xattn_Wq"]).reshape(PAIRS + 1, DC, P, P).transpose(0, 2, 1, 3),
        "w_o": a["L0_xattn_Wo"].reshape(PAIRS, P, D),
        "bo": a["L0_xattn_bo"],
        "w_sq": w_attn[:, 0:D],
        "w_sk": np.concatenate([w_attn[:, D:D + SHD]] * SH8, axis=1),
        "w_sv": w_attn[:, D + SHD:D + 2 * SHD],
        "w_proj": a["L0_attn_w_proj"],
        "router_w": a["L0_ffn_router_w"],
        "router_b": a["L0_ffn_router_b"],
        "w1": np.concatenate([a["L0_ffn_routed_w1"], a["L0_ffn_shared_w1"]], axis=0),
        "w3": np.concatenate([a["L0_ffn_routed_w3"], a["L0_ffn_shared_w3"]], axis=0),
        "w2": np.concatenate([a["L0_ffn_routed_w2"], a["L0_ffn_shared_w2"]], axis=0),
    }
    arrays = {f"in_{k}": np.ascontiguousarray(v) for k, v in arrays.items()}
    nc = _bacc.Bacc("TRN2", target_bir_lowering=False, num_devices=1)
    args = [nc.dram_tensor(k, v.shape, _mybir.dt.from_np(v.dtype), kind="ExternalInput").ap() for k, v in arrays.items()]
    out = nc.dram_tensor("out", (N, D), F32, kind="ExternalOutput").ap()
    build(nc, *args, out)
    r = _run(nc, [arrays], core_ids=[0])
    return r.results[0]["out"].reshape(1, N, D)
```
